# Optimizing a Trainium2 kernel written in Bass

```python
import numpy as np
import jax
import jax.numpy as jnp

def _softmax(x, axis=-1):
    return jax.nn.softmax(x, axis=axis)

def _gelu(x):
    return jax.nn.gelu(x, approximate=True)

def _silu(x):
    return jax.nn.silu(x)

def _sigmoid(x):
    return jax.nn.sigmoid(x)

def _layernorm(x, axis=-1, eps=1e-05):
    m = jnp.mean(x, axis=axis, keepdims=True)
    v = jnp.var(x, axis=axis, keepdims=True)
    return (x - m) / jnp.sqrt(v + eps)

def _scatter_add(tgt, idx, src, axis=0):
    return tgt.at[idx].add(src)

def _segment_sum(src, seg, n):
    return jax.ops.segment_sum(src, seg, n)
kernel_name = 'mk_gnn_ffn_d2_gnn_r32_72ac20'

def setup_inputs(seed: int=0):
    np.random.seed(seed)
    _w = jnp.asarray

    def _rec_inputs():
        import jax
        import jax.numpy as jnp
        _gk = jax.random.key(seed)
        x = -8.776e-05 + 1 * jax.random.normal(jax.random.fold_in(_gk, 1), (3125, 256), jnp.float32)
        src = jax.random.randint(jax.random.fold_in(_gk, 2), (50000,), 0, 3125, jnp.int32)
        dst = jax.random.randint(jax.random.fold_in(_gk, 3), (50000,), 0, 3125, jnp.int32)
        _o = jnp.argsort(dst, stable=True)
        src = src[_o]
        dst = dst[_o]
        edge_type_8 = jax.random.randint(jax.random.fold_in(_gk, 13), (50000,), 0, 8, jnp.int32)
        return (x, src, dst, edge_type_8)
    x, src, dst, edge_type_8 = _rec_inputs()

    def _L0_gnn_setup():
        import jax, jax.numpy as jnp
        import numpy as np
        N_NODES = 625
        N_EDGES = 10000
        IN_DIM = 256
        OUT_DIM = 256
        NUM_RELS = 8
        NUM_BASES = 4
        key = jax.random.key(seed)
        k = jax.random.split(key, 7)
        return {'h': jax.random.normal(k[0], (N_NODES, IN_DIM), dtype=jnp.float32), 'basis': jax.random.normal(k[1], (NUM_BASES, IN_DIM, OUT_DIM), dtype=jnp.float32) * (6.0 / (IN_DIM + OUT_DIM)) ** 0.5, 'w_comp': jax.random.normal(k[2], (NUM_RELS, NUM_BASES), dtype=jnp.float32), 'bias': jax.random.normal(k[3], (OUT_DIM,), dtype=jnp.float32) * 0.01, 'src': jax.random.randint(k[4], (N_EDGES,), 0, N_NODES, dtype=jnp.int32), 'dst': jax.random.randint(k[5], (N_EDGES,), 0, N_NODES, dtype=jnp.int32), 'etype': jax.random.randint(k[6], (N_EDGES,), 0, NUM_RELS, dtype=jnp.int32)}
    _L0_gnn_all = _L0_gnn_setup()
    _L0_gnn_in = {k: v for k, v in _L0_gnn_all.items() if k in ('basis', 'w_comp', 'bias')}
    del _L0_gnn_all

    def _L0_ffn_setup():
        import jax, jax.numpy as jnp
        import numpy as np
        N_EXPERTS = 8
        TOP_K = 2
        key = jax.random.key(seed)
        ks = jax.random.split(key, 5)
        B, T, C, E, H = (8, 64, 256, 8, 682)
        scale = 1.0 / np.sqrt(C)
        return {'x': jax.random.normal(ks[0], (B, T, C), dtype=jnp.float32), 'router_w': jax.random.normal(ks[1], (E, C), dtype=jnp.float32) * scale, 'w1': jax.random.normal(ks[2], (E, H, C), dtype=jnp.float32) * scale, 'w2': jax.random.normal(ks[3], (E, C, H), dtype=jnp.float32) * (1.0 / np.sqrt(H)), 'w3': jax.random.normal(ks[4], (E, H, C), dtype=jnp.float32) * scale}
    _L0_ffn_all = _L0_ffn_setup()
    _L0_ffn_in = {k: v for k, v in _L0_ffn_all.items() if k in ('router_w', 'w1', 'w2', 'w3')}
    del _L0_ffn_all

    def _L1_gnn_setup():
        import jax, jax.numpy as jnp
        import numpy as np
        N_NODES = 10000
        N_EDGES = 5000
        D = 256
        P = 2.0
        key = jax.random.key(seed)
        k1, k2, k3, k4 = jax.random.split(key, 4)
        X = jax.random.normal(k1, (N_NODES, D), dtype=jnp.float32)
        edge_index = jax.random.randint(k2, (2, N_EDGES), 0, N_NODES, dtype=jnp.int64)
        scale = 1.0 / np.sqrt(D)
        W_root = jax.random.normal(k3, (D, D), dtype=jnp.float32) * scale
        W_neigh = jax.random.normal(k4, (D, D), dtype=jnp.float32) * scale
        b = jnp.zeros((D,), dtype=jnp.float32)
        return {'X': X, 'edge_index': edge_index, 'W_root': W_root, 'W_neigh': W_neigh, 'b': b}
    _L1_gnn_all = _L1_gnn_setup()
    _L1_gnn_in = {k: v for k, v in _L1_gnn_all.items() if k in ('W_root', 'W_neigh', 'b')}
    del _L1_gnn_all

    def _L1_ffn_setup():
        import jax, jax.numpy as jnp
        import numpy as np
        NUM_EXPERTS = 8
        TOP_K = 2
        B, S, D = (8, 256, 256)

        def _moe(tokens, router_w, w1, b1, w2, b2):
            N = tokens.shape[0]
            E = router_w.shape[0]
            logits = tokens.astype(jnp.float32) @ router_w.astype(jnp.float32).T
            probs = jax.nn.softmax(logits, axis=-1)
            rw, re = jax.lax.top_k(probs, TOP_K)
            if TOP_K > 1:
                rw = rw / jnp.maximum(rw.sum(-1, keepdims=True), 1e-12)
            rw = rw.astype(tokens.dtype)
            combine = jnp.zeros((N, E), tokens.dtype).at[jnp.arange(N)[:, None], re].set(rw)
            out = tokens
            for e in range(E):
                h = jax.nn.gelu(tokens @ w1[e] + b1[e], approximate=False)
                y = h @ w2[e] + b2[e]
                out = out + combine[:, e:e + 1] * y
            return out
        key = jax.random.key(seed)
        ks = jax.random.split(key, 4)
        scale = 1.0 / np.sqrt(D).astype(np.float32)
        return {'input_embeddings': jax.random.normal(ks[0], (B, S, D), jnp.float32), 'router_w': jax.random.normal(ks[1], (NUM_EXPERTS, D), jnp.float32) * scale, 'w1': jax.random.normal(ks[2], (NUM_EXPERTS, D, D), jnp.float32) * scale, 'b1': jnp.zeros((NUM_EXPERTS, D), jnp.float32), 'w2': jax.random.normal(ks[3], (NUM_EXPERTS, D, D), jnp.float32) * scale, 'b2': jnp.zeros((NUM_EXPERTS, D), jnp.float32)}
    _L1_ffn_all = _L1_ffn_setup()
    _L1_ffn_in = {k: v for k, v in _L1_ffn_all.items() if k in ('router_w', 'w1', 'b1', 'w2', 'b2')}
    del _L1_ffn_all
    return {'x': x, 'src': src, 'dst': dst, 'edge_type_8': edge_type_8, 'L0_gnn_basis': _L0_gnn_in['basis'], 'L0_gnn_w_comp': _L0_gnn_in['w_comp'], 'L0_gnn_bias': _L0_gnn_in['bias'], 'L0_ffn_router_w': _L0_ffn_in['router_w'], 'L0_ffn_w1': _L0_ffn_in['w1'], 'L0_ffn_w2': _L0_ffn_in['w2'], 'L0_ffn_w3': _L0_ffn_in['w3'], 'L1_gnn_W_root': _L1_gnn_in['W_root'], 'L1_gnn_W_neigh': _L1_gnn_in['W_neigh'], 'L1_gnn_b': _L1_gnn_in['b'], 'L1_ffn_router_w': _L1_ffn_in['router_w'], 'L1_ffn_w1': _L1_ffn_in['w1'], 'L1_ffn_b1': _L1_ffn_in['b1'], 'L1_ffn_w2': _L1_ffn_in['w2'], 'L1_ffn_b2': _L1_ffn_in['b2']}

def reference(x, src, dst, edge_type_8, L0_gnn_basis, L0_gnn_w_comp, L0_gnn_bias, L0_ffn_router_w, L0_ffn_w1, L0_ffn_w2, L0_ffn_w3, L1_gnn_W_root, L1_gnn_W_neigh, L1_gnn_b, L1_ffn_router_w, L1_ffn_w1, L1_ffn_b1, L1_ffn_w2, L1_ffn_b2):
    import jax
    import jax.numpy as jnp

    def _L0_gnn_ref(h, basis, w_comp, bias, src, dst, etype):
        import jax, jax.numpy as jnp
        import numpy as np
        N_NODES = 625
        N_EDGES = 10000
        IN_DIM = 256
        OUT_DIM = 256
        NUM_RELS = 8
        NUM_BASES = 4
        in_dim, out_dim = (h.shape[1], basis.shape[2])
        num_rels = w_comp.shape[0]
        wr = basis.reshape(in_dim, NUM_BASES, out_dim)
        weight = jnp.einsum('rb,ibo->iro', w_comp, wr)
        weight = weight.reshape(num_rels, in_dim, out_dim)
        t = jnp.einsum('nd,rdo->rno', h, weight)
        msg = t[etype, src]
        agg = jax.ops.segment_sum(msg, dst, num_segments=h.shape[0])
        return jax.nn.relu(agg + bias)

    def _L0_ffn_ref(x, router_w, w1, w2, w3):
        import jax, jax.numpy as jnp
        import numpy as np
        N_EXPERTS = 8
        TOP_K = 2
        B, T, C = x.shape
        flat = x.reshape(-1, C)
        logits = flat @ router_w.T
        probs = jax.nn.softmax(logits, axis=-1)
        topk_probs, topk_idx = jax.lax.top_k(probs, TOP_K)
        topk_probs = topk_probs / (jnp.sum(topk_probs, axis=-1, keepdims=True) + 1e-09)
        onehot = jax.nn.one_hot(topk_idx, N_EXPERTS, dtype=flat.dtype)
        gates = jnp.einsum('nk,nke->ne', topk_probs, onehot)
        h1 = jnp.einsum('nc,ehc->neh', flat, w1)
        h3 = jnp.einsum('nc,ehc->neh', flat, w3)
        h = jax.nn.silu(h1) * h3
        y = jnp.einsum('neh,ech->nec', h, w2)
        out = jnp.einsum('ne,nec->nc', gates, y)
        return out.reshape(B, T, C)

    def _L1_gnn_ref(X, edge_index, W_root, W_neigh, b):
        import jax, jax.numpy as jnp
        import numpy as np
        N_NODES = 10000
        N_EDGES = 5000
        D = 256
        P = 2.0
        n = X.shape[0]
        row, col = (edge_index[0], edge_index[1])
        ones = jnp.ones((row.shape[0],), dtype=X.dtype)
        deg = jax.ops.segment_sum(ones, row, num_segments=n)
        denom = jnp.maximum(deg, 1.0)[:, None]
        neigh_sum = jax.ops.segment_sum(X[col], row, num_segments=n)
        neigh_mean = neigh_sum / denom
        H = jax.nn.relu(X @ W_root + neigh_mean @ W_neigh + b)
        diffs = jnp.abs(H[row] - H[col]) ** P
        gg = jax.ops.segment_sum(diffs, row, num_segments=n) / denom
        return jnp.tanh(gg)

    def _L1_ffn_ref(input_embeddings, router_w, w1, b1, w2, b2):
        import jax, jax.numpy as jnp
        import numpy as np
        NUM_EXPERTS = 8
        TOP_K = 2
        B, S, D = (8, 256, 256)

        def _moe(tokens, router_w, w1, b1, w2, b2):
            N = tokens.shape[0]
            E = router_w.shape[0]
            logits = tokens.astype(jnp.float32) @ router_w.astype(jnp.float32).T
            probs = jax.nn.softmax(logits, axis=-1)
            rw, re = jax.lax.top_k(probs, TOP_K)
            if TOP_K > 1:
                rw = rw / jnp.maximum(rw.sum(-1, keepdims=True), 1e-12)
            rw = rw.astype(tokens.dtype)
            combine = jnp.zeros((N, E), tokens.dtype).at[jnp.arange(N)[:, None], re].set(rw)
            out = tokens
            for e in range(E):
                h = jax.nn.gelu(tokens @ w1[e] + b1[e], approximate=False)
                y = h @ w2[e] + b2[e]
                out = out + combine[:, e:e + 1] * y
            return out
        b, s, d = input_embeddings.shape
        tokens = input_embeddings.reshape(b * s, d)
        return _moe(tokens, router_w, w1, b1, w2, b2).reshape(b, s, d)
    edge_index = jnp.stack([src, dst])
    x = x + _L0_gnn_ref(_layernorm(x, axis=-1), L0_gnn_basis, L0_gnn_w_comp, L0_gnn_bias, src, dst, edge_type_8)
    x = x + _L0_ffn_ref(_layernorm(x, axis=-1)[None], L0_ffn_router_w, L0_ffn_w1, L0_ffn_w2, L0_ffn_w3)[0]
    x = x + _L1_gnn_ref(_layernorm(x, axis=-1), edge_index, L1_gnn_W_root, L1_gnn_W_neigh, L1_gnn_b)
    x = x + _L1_ffn_ref(_layernorm(x, axis=-1)[None], L1_ffn_router_w, L1_ffn_w1, L1_ffn_b1, L1_ffn_w2, L1_ffn_b2)[0]
    return x

_drawn_inputs = setup_inputs


def setup_inputs(seed=0):
    import zlib

    import numpy as np

    out = dict(_drawn_inputs(seed))
    spreads = {'L1_gnn_b': (0.0, 0.8), 'L1_ffn_b1': (0.0, 0.8), 'L1_ffn_b2': (0.0, 0.8)}
    factors = {'L0_gnn_bias': 8.0, 'L1_gnn_W_neigh': 5.181}
    for name, (base, spread) in spreads.items():
        noise = np.random.default_rng([zlib.crc32(name.encode()), seed]).standard_normal(out[name].shape)
        drawn = base * np.exp(spread * noise) if base else spread * noise
        out[name] = jnp.asarray(drawn.astype(out[name].dtype))
    for name, factor in factors.items():
        out[name] = (out[name] * factor).astype(out[name].dtype)
    return out
```

```python
from contextlib import ExitStack

import concourse.bass as bass
from concourse import mybir

F32 = mybir.dt.float32
I32 = mybir.dt.int32
ALU = mybir.AluOpType
ACT = mybir.ActivationFunctionType
AX_X = mybir.AxisListType.X

P = 128
N, D = 3125, 256
T = -(-N // P)
NP = T * P
E = 50000
C = 392
NREL, NBASES = 8, 4
KS = 416
X, TOPK = 8, 2
H0 = 682
HH = H0 // 2
HC = 114
NHC = -(-H0 // HC)
CM = TOPK * T
KM = 56
EPS = 1e-5
SKIP = 1.0e6
PACK = 32768
SB = 14
GBS = (8, 4, 4)
NLN = 4
BG = 10
assert C * P >= E and C % (2 * SB) == 0 and all(KS % (2 * g) == 0 for g in GBS)
assert KS >= (E + T * (P - 1)) // P and KM >= (N * TOPK + X * (P - 1)) // P and T % 2 and KM % 2 == 0
assert P * PACK + N * NREL < 1 << 24 and NP * NREL <= PACK


def program(nc, a, out):
    rel_table = nc.dram_tensor("rel_table", [NP * NREL, D], F32)
    x_table = nc.dram_tensor("x_table", [NP, D], F32)
    h_table = nc.dram_tensor("h_table", [NP, D], F32)
    sorted_edges = [nc.dram_tensor(f"sorted_edges{l}", [P * KS, 1], I32) for l in range(2)]
    tok_in = nc.dram_tensor("tok_in", [KM * P, D], F32)
    tok_out = nc.dram_tensor("tok_out", [KM * P, D], F32)

    with ExitStack() as ctx:
        def sb(name, shape, dt=F32):
            return ctx.enter_context(nc.sbuf_tensor(name, shape, dt))

        def sem(name):
            return ctx.enter_context(nc.semaphore(name))

        x = sb("x", [P, T, D])
        hn = sb("hn", [P, T, D])
        consts = sb("consts", [P, 3 * P])
        ident, below, lane = (consts[:, i * P:(i + 1) * P] for i in range(3))
        ones = sb("ones", [P, P])
        small = sb("small", [P, T + 2 * X + T])
        iota_t, iota_x, iota_x8 = small[:, 0:T], small[:, T:T + X], small[:, T + X:T + 2 * X]
        beyond = small[:, T + 2 * X:2 * T + 2 * X]
        starts = sb("starts", [1, KS])
        bias0 = sb("bias0", [P, D])
        bias1 = sb("bias1", [P, D])
        rw = sb("rw", [P, 2, 2, X])
        wc = sb("wc", [P, NBASES])
        gidx = sb("gidx", [P, KS], I32)
        lists = sb("lists", [P, 2 * KS], I32)
        packed, gloc_i = lists[:, 0:KS], lists[:, KS:2 * KS]
        lg = lists[:, 0:4 * T * X].bitcast(F32).rearrange("p (i t e) -> p i t e", i=4, t=T)
        gloc = sb("gloc", [P, KS])
        sort_work = sb("sort_work", [P, 2 * X * CM])
        bucket = sort_work[:, 0:2 * C].rearrange("p (l c) -> p l c", l=2)
        msort = sort_work[:, :].rearrange("p (i e c) -> p i e c", i=2, e=X)
        place = sb("place", [P, 2, C], I32)
        load = sb("load", [P, 2, C], I32)
        block_of = sb("block_of", [1, 2, KS], I32)
        expert_of = sb("expert_of", [1, KM], I32)
        stg_place = sb("stg_place", [P, 2, SB], I32)
        stg_load = sb("stg_load", [P, 2, SB], I32)
        stg_g = sb("stg_g", [P, 2, max(GBS)], I32)
        stats = sb("stats", [P, T, 6])
        mean = sb("mean", [P, T])
        rstd = sb("rstd", [P, T])
        upto = sb("upto", [P, T + 1])
        cnt = sb("cnt", [P, 4, T])
        cnt_i = sb("cnt_i", [P, T], I32)
        hT = sb("hT", [P, 2, 2, P])
        gates = sb("gates", [P, TOPK, T])
        tops = sb("tops", [P, 2, T])
        choice = sb("choice", [P, TOPK, T])
        rank = sb("rank", [P, CM])
        tplace = sb("tplace", [P, 2, CM], I32)
        deg = sb("deg", [P, 2, T])

        ARENA = 4 * X * H0 + (NHC - 1) * X * D
        arena = sb("arena", [P, ARENA])

        def at(off, *shape, dt=F32, parts=P):
            n = 1
            for d in shape:
                n *= d
            assert off + n <= ARENA
            v = arena[0:parts, off:off + n]
            if dt != F32:
                v = v.bitcast(dt)
            names = "abc"[:len(shape)]
            if len(shape) > 1:
                v = v.rearrange(f"p ({' '.join(names)}) -> p {' '.join(names)}", **dict(zip(names[:-1], shape)))
            return v

        hot_sort, scan_sort = at(0, T, C), at(T * C, T, C)
        hot_flat, scan_flat = at(0, T * C), at(T * C, T * C)
        basis_sb = at(0, NREL, NBASES, D)
        w_rel = at(2 * T * C, 2, NREL, D)
        o = 2 * T * C + 2 * NREL * D
        rel_out = at(o, 2, NREL * D)
        raw = at(o, 3, C, dt=I32)
        work_i = at(o + 3 * C, 3, C, dt=I32)
        work_f = at(o + 6 * C, 2, C)
        w13 = at(0, 4, X * H0)
        o = 4 * X * H0
        gath = [at(o, 2 * GBS[0], D)]
        hot = [at(o + 2 * GBS[0] * D, 2 * GBS[0], P)]
        w2a = at(o, NHC - 1, X * D)
        acc0 = hn
        hnf = hn[:, :, :].rearrange("p a b -> p (a b)")
        xs = hnf[:, 0:512].rearrange("p (j d) -> p j d", j=2)
        xsT = hnf[:, 512:1024].rearrange("p (j k d) -> p j k d", j=2, k=2)
        ys = hnf[:, 1024:1536].rearrange("p (j d) -> p j d", j=2)
        hid = hnf[:, 1536:1536 + H0]
        hidT = hnf[:, 2304:2304 + 2 * NHC * P].rearrange("p (j k d) -> p j k d", j=2, k=NHC)
        w2b = hnf[:, 4096:4096 + X * D]
        w2 = [w2a[:, k, :] for k in range(NHC - 1)] + [w2b]
        y_back = at(0, CM, D)
        root = at(0, T, D)
        accx = at(T * D, T, D + 1)
        o = T * (2 * D + 1)
        acch = at(o, T, 2 * D)
        o += T * 2 * D
        gath.append(at(o, 2 * GBS[1], 2 * D))
        hot.append(at(o + 4 * GBS[1] * D, 2 * GBS[1], P))
        gath.append(gath[1])
        hot.append(hot[1])
        o += 2 * GBS[1] * (2 * D + P)
        w_root, w_neigh = at(o, 2, D), at(o + 2 * D, 2, D)
        e1w1, e1w2 = at(CM * D, 2, X * D), at(CM * D + 2 * X * D, 2, X * D)
        e1b = at(CM * D + 4 * X * D, 2, X * D, parts=1)
        acc = [acc0[:, :, :], accx, acch]
        width = [D, D + 1, 2 * D]

        ps = ctx.enter_context(nc.psum_tensor("ps", [P, 8, 512], F32))

        edges_in, consts_in, x_in, wc_in, bias_in, rw_in = map(
            sem, "edges_in consts_in x_in wc_in bias_in rw_in".split())
        basis_in = [sem("basis_in0"), sem("basis_in1")]
        basis_used, set_pool, pad_set, zero_set, lists_init, tok_init = map(
            sem, "basis_used set_pool pad_set zero_set lists_init tok_init".split())
        dve_step, ranked, counted, edges_placed, tokens_placed = map(
            sem, "dve_step ranked counted edges_placed tokens_placed".split())
        staged, list_in, list_ready = map(sem, "staged list_in list_ready".split())
        scattered = [sem("scattered0"), sem("scattered1")]
        stat_out = sem("stat_out")
        var_out, std_out, normed, turned, turned_in, routed = map(
            sem, "var_out std_out normed turned turned_in routed".split())
        w_rel_out, rel_mm, rel_act, rel_dve = map(sem, "w_rel_out rel_mm rel_act rel_dve".split())
        rel_stored = [sem("rel_stored0"), sem("rel_stored1")]
        gathered = [[sem(f"gathered{l}_{b}") for b in range(2 * GBS[l])] for l in range(3)]
        hot_out = [sem(f"hot_out{l}") for l in range(3)]
        summed = [sem(f"summed{l}") for l in range(3)]
        added = [sem(f"added{l}") for l in range(3)]
        squared, acc_zero = sem("squared"), sem("acc_zero")
        w13_in, w2_in, e1_in, wl_in = map(sem, "w13_in w2_in e1_in wl_in".split())
        lgm_out, exp_out, sent = map(sem, "lgm_out exp_out sent".split())
        xs_in = [sem("xs_in0"), sem("xs_in1")]
        xs_turned, xsT_in, h_mm, act_out, hid_out, hid_turned, hidT_act, hidT_dve, y_mm, y_out = map(
            sem, "xs_turned xsT_in h_mm act_out hid_out hid_turned hidT_act hidT_dve y_mm y_out".split())
        ys_stored = [sem("ys_stored0"), sem("ys_stored1")]
        back = [sem(f"back{g}") for g in range(CM // BG)]
        combined, combined_all, x_stored, root_mm, root_out, mean_out, neigh_mm, pre_out, h_out, h_stored = map(
            sem, "combined combined_all x_stored root_mm root_out mean_out neigh_mm pre_out h_out h_stored".split())
        gg_out, tanh_out, graph_done, out_stored = map(sem, "gg_out tanh_out graph_done out_stored".split())
        passed = {e: sem(f"passed_{e}") for e in ("sp", "pool", "act", "dve", "pe")}

        def hold(e, eng, semaphore, value):
            if isinstance(value, int):
                if value > 0:
                    eng.wait_ge(semaphore, value)
            else:
                eng.wait_ge(semaphore, value)
                eng.sem_inc(passed[e], 1)

        def pairs(eng, body):
            for t in range(3):
                body(t, t % 2)
            with eng.Fori(1, T // 2) as i:
                body(i * 2 + 1, 1)
                body(i * 2 + 2, 0)

        def rounds(eng, n, body):
            body(0)
            with eng.Fori(1, n) as i:
                body(i)

        block = ctx.enter_context(nc.Block())

        @block.sync
        def _(sp):
            full = (T - 1) * P
            for i, name in enumerate(("src", "dst", "et")):
                sp.dma_start(raw[:, i, :], a[name]).then_inc(edges_in, 16)
            sp.dma_start(consts[:, :], a["c_mats"]).then_inc(consts_in, 16)
            sp.dma_start(small[:, :], a["c_small"]).then_inc(consts_in, 16)
            sp.dma_start(starts[:, :], a["c_starts"]).then_inc(consts_in, 16)
            sp.wait_ge(zero_set, 1)
            sp.dma_start(x[:, 0:T - 1, :], a["x"][0:full, :].rearrange("(t p) d -> p t d", p=P)
                         ).then_inc(x_in, 16)
            sp.dma_start(x[0:N - full, T - 1, :], a["x"][full:N, :]).then_inc(x_in, 16)
            for r in range(NREL):
                sp.dma_start(wc[r::NREL, :], a["w_comp"][r:r + 1, :].to_broadcast([P // NREL, NBASES])
                             ).then_inc(wc_in, 16)
            for name, b in (("bias0", bias0), ("bias1", bias1)):
                sp.dma_start(b[:, :], a[name].to_broadcast([P, D])).then_inc(bias_in, 16)
            sp.dma_start(rw[:, :, :, :], a["rw"]).then_inc(rw_in, 16)
            sp.wait_ge(pad_set, 2)
            for l, pad in ((0, packed), (1, gloc_i)):
                sp.dma_start(sorted_edges[l][:, :].rearrange("(p k) o -> p (k o)", p=P), pad
                             ).then_inc(lists_init, 16)
            sp.wait_ge(zero_set, 2)
            rows = 8
            tok_p = tok_in[:, :].rearrange("(p r) d -> p (r d)", p=P)
            for q in range(KM // rows):
                sp.dma_start(tok_p[:, q * rows * D:(q + 1) * rows * D], hnf[:, 0:rows * D]).then_inc(tok_init, 16)
            bases = a["basis"].rearrange("(s q b) o -> q s (b o)", q=P // 4, b=NBASES)
            sp.wait_ge(edges_placed, 1)
            for k in range(2):
                if k:
                    sp.wait_ge(basis_used, 1)
                for r in range(NREL):
                    sp.dma_start(basis_sb[r::NREL, :, :, :].rearrange("p a b c -> p a (b c)"),
                                 bases[k * P // NREL:(k + 1) * P // NREL]).then_inc(basis_in[k], 16)

            def store_rel(t, j):
                hold("sp", sp, rel_act, t * 2 + 2)
                hold("sp", sp, rel_dve, t * 2 + 2)
                sp.dma_start(rel_table[bass.ds(t * (P * NREL), P * NREL), :].rearrange("(p r) d -> p (r d)", r=NREL),
                             rel_out[:, j, :]).then_inc(rel_stored[j], 16)
            pairs(sp, store_rel)

            sp.wait_ge(edges_placed, 2)
            sp.wait_ge(rel_mm, 4 * T)
            for i, name in enumerate(("w1", "w1", "w3", "w3")):
                sp.dma_start(w13[:, i, :].rearrange("p (e h) -> p e h", e=X),
                             a[name][:, (i % 2) * P:(i % 2 + 1) * P, :].rearrange("e c h -> c e h")).then_inc(w13_in, 16)

            def load_list(l):
                for h in range(2):
                    sp.wait_ge(scattered[h], 16 * (C // 2) * (l + 1))
                sp.dma_start(packed, sorted_edges[l][:, :].rearrange("(p k) o -> p (k o)", p=P)
                             ).then_inc(list_in, 16)
            load_list(0)
            sp.wait_ge(added[0], KS)
            for k in range(NHC):
                n = min(HC, H0 - k * HC)
                if k == NHC - 1:
                    sp.wait_ge(sent, 16 * CM)
                sp.dma_start(w2[k][0:n, :].rearrange("p (e d) -> p e d", e=X),
                             a["w2"][:, k * HC:k * HC + n, :].rearrange("e h d -> h e d")).then_inc(w2_in, 16)

            def slots(l):
                sp.wait_ge(sent, 16 * CM * (l + 1))

                def store(i, j):
                    hold("sp", sp, y_out, i * 2 + (j + 1 + l * KM))
                    sp.dma_start(tok_out[bass.ds((i * 2 + j) * P, P), :], ys[:, j, :]).then_inc(ys_stored[j], 16)

                def body(i):
                    for j in range(2):
                        if not isinstance(i, int):
                            hold("sp", sp, xs_turned, i * 2 + (j - 1 + l * KM))
                        sp.dma_start(xs[:, j, :], tok_in[bass.ds((i * 2 + j) * P, P), :]).then_inc(xs_in[j], 16)
                    for j in range(2):
                        if not isinstance(i, int):
                            store(i - 1, j)
                rounds(sp, KM // 2, body)
                for j in range(2):
                    store(KM // 2 - 1, j)
            slots(0)
            load_list(1)
            sp.wait_ge(combined_all, 1)
            for name, w in (("W_root", w_root), ("W_neigh", w_neigh)):
                sp.dma_start(w, a[name].rearrange("(k p) d -> p k d", p=P)).then_inc(wl_in, 16)
            sp.wait_ge(normed, 3 * T)
            sp.dma_start(x_table[:, :].rearrange("(t p) d -> p t d", p=P), hn[:, :, :]).then_inc(x_stored, 16)
            sp.wait_ge(h_out, T)
            sp.dma_start(h_table[:, :].rearrange("(t p) d -> p t d", p=P), root).then_inc(h_stored, 16)
            sp.wait_ge(graph_done, 1)
            for k in range(2):
                for name, w in (("e1w1", e1w1), ("e1w2", e1w2)):
                    sp.dma_start(w[:, k, :].rearrange("p (e h) -> p e h", e=X),
                                 a[name][:, k * P:(k + 1) * P, :].rearrange("e c h -> c e h")).then_inc(e1_in, 16)
                sp.dma_start(e1b[:, k, :], a[f"e1b{k + 1}"]).then_inc(e1_in, 16)
            slots(1)
            sp.wait_ge(combined_all, 2)
            sp.dma_start(out[0:full, :].rearrange("(t p) d -> p t d", p=P), x[:, 0:T - 1, :]).then_inc(out_stored, 16)
            sp.dma_start(out[full:N, :], x[0:N - full, T - 1, :]).then_inc(out_stored, 16)
            sp.wait_ge(out_stored, 32)

        @block.gpsimd
        def _(pool):
            pool.memset(x[:, T - 1, :], 0.0).then_inc(zero_set, 1)
            pool.memset(hnf[:, 0:8 * D], 0.0).then_inc(zero_set, 1)
            pool.memset(ones[:, :], 1.0).then_inc(set_pool, 1)
            pool.memset(packed, P * PACK + N * NREL).then_inc(pad_set, 1)
            pool.memset(gloc_i, P * PACK + N).then_inc(pad_set, 1)
            halves = [0]

            def scatter_edges(l):
                pool.wait_ge(edges_placed, l + 1)
                base = halves[0]

                def body(i):
                    for h in range(2):
                        hold("pool", pool, scattered[h], (i + l * (C // SB // 2)) * (16 * SB))
                        at_ = bass.ds((i * 2 + h) * SB, SB)
                        pool.tensor_copy(stg_place[:, h, :], place[:, l, at_]).then_inc(staged, 1)
                        pool.tensor_copy(stg_load[:, h, :], load[:, l, at_]).then_inc(staged, 1)
                        hold("pool", pool, staged, (i * 2 + h + 1) * 2 + base)
                        for b in range(SB):
                            pool.indirect_dma_start(
                                sorted_edges[l][:, :], bass.IndirectOffsetOnAxis(ap=stg_place[:, h, b:b + 1], axis=0),
                                stg_load[:, h, b:b + 1], None, bounds_check=P * KS - 1, oob_is_err=False,
                            ).then_inc(scattered[h], 16)
                rounds(pool, C // SB // 2, body)
                halves[0] += C // SB * 2

            def gather(l, table):
                base, gb = halves[0], GBS[l]

                def body(i):
                    for h in range(2):
                        hold("pool", pool, summed[l], max((i * 2 + h - 1) * gb, 0) if isinstance(i, int)
                             else i * (2 * gb) + (h - 1) * gb)
                        pool.tensor_copy(stg_g[:, h, 0:gb], gidx[:, bass.ds((i * 2 + h) * gb, gb)]).then_inc(staged, 1)
                        hold("pool", pool, staged, i * 2 + (h + 1 + base))
                        for b in range(gb):
                            pool.indirect_dma_start(
                                gath[l][:, h * gb + b, 0:D], None, table[:, :],
                                bass.IndirectOffsetOnAxis(ap=stg_g[:, h, b:b + 1], axis=0),
                            ).then_inc(gathered[l][h * gb + b], 16)
                rounds(pool, KS // gb // 2, body)
                halves[0] += KS // gb

            def send_tokens(l):
                pool.wait_ge(tokens_placed, l + 1)
                for c in range(CM):
                    pool.indirect_dma_start(
                        tok_in[:, :], bass.IndirectOffsetOnAxis(ap=tplace[:, 0, c:c + 1], axis=0),
                        hn[:, c % T, :], None, bounds_check=KM * P - 1, oob_is_err=False).then_inc(sent, 16)

            def bring_back(l):
                for j in range(2):
                    pool.wait_ge(ys_stored[j], 16 * (KM // 2) * (l + 1))
                for c in range(CM):
                    pool.indirect_dma_start(
                        y_back[:, c, :], None, tok_out[:, :],
                        bass.IndirectOffsetOnAxis(ap=tplace[:, 1, c:c + 1], axis=0)).then_inc(back[c // BG], 16)

            pool.wait_ge(lists_init, 32)
            scatter_edges(0)
            pool.wait_ge(list_ready, 1)
            pool.wait_ge(rel_stored[0], 16 * (T // 2 + 1))
            pool.wait_ge(rel_stored[1], 16 * (T // 2))
            gather(0, rel_table)
            pool.wait_ge(tok_init, 16 * KM // 8)
            send_tokens(0)
            scatter_edges(1)
            bring_back(0)
            pool.wait_ge(list_ready, 2)
            pool.wait_ge(x_stored, 16)
            gather(1, x_table)
            pool.wait_ge(h_stored, 16)
            gather(2, h_table)
            send_tokens(1)
            bring_back(1)

        @block.scalar
        def _(act):
            def std(n):
                act.wait_ge(var_out, n)
                act.activation(rstd[:, :], rstd[:, :], ACT.Sqrt).then_inc(std_out, 1)

            def turn(n, used, per=1, base=0):
                def body(t, j):
                    hold("act", act, turned, t + (n * T + 1))
                    if not isinstance(t, int) or t >= 2:
                        hold("act", act, used, (t - 1) * per + base)
                    act.copy(hT[:, j, :, :].rearrange("p k d -> p (k d)"), ps[:, 6 + j, 0:D]).then_inc(turned_in, 1)
                return body

            def rel_part(t, j):
                turn(0, rel_mm, 4)(t, j)
                hold("act", act, rel_stored[j], (t - j) * 8)
                for n, g in enumerate((0, 2)):
                    hold("act", act, rel_mm, t * 4 + g + 1)
                    act.copy(rel_out[:, j, g * 512:(g + 1) * 512], ps[:, g, :]).then_inc(rel_act, 1)

            def softmax_exp(n):
                act.wait_ge(lgm_out, n)
                act.activation(lg[:, 1, :, :], lg[:, 1, :, :], ACT.Exp).then_inc(exp_out, 1)

            def experts(l):
                g = l * KM

                def xsT_copy(k, j):
                    hold("act", act, xs_turned, k + (g + 1))
                    hold("act", act, h_mm, k + (g - 1))
                    act.copy(xsT[:, j, :, :].rearrange("p k d -> p (k d)"), ps[:, 5, 0:D]).then_inc(xsT_in, 1)

                def slot(k, j, last=False):
                    hold("act", act, h_mm, k + (g + 1))
                    if l == 0:
                        hold("act", act, hid_turned, k)
                        act.activation(hid.rearrange("p (b h) -> p b h", b=2), ps[:, 0:2, 0:HH], ACT.Silu
                                       ).then_inc(act_out, 1)
                    else:
                        hold("act", act, hid_turned, k + g)
                        act.activation(hid[:, 0:D], ps[:, 0, 0:D], ACT.Gelu).then_inc(hid_out, 1)
                    if not last:
                        xsT_copy(k + 1, 1 - j)
                    hold("act", act, hid_turned, k + (g + 1))
                    hold("act", act, y_mm, k + (g - 1))
                    if l == 0:
                        act.copy(hidT[0:HC, j, 0:4, :], ps[0:HC, 6, :].rearrange("p (k d) -> p k d", k=4)
                                 ).then_inc(hidT_act, 1)
                    else:
                        act.copy(hidT[:, j, 0:2, :], ps[:, 6, 0:D].rearrange("p (k d) -> p k d", k=2)
                                 ).then_inc(hidT_act, 1)

                xsT_copy(0, 0)
                slot(0, 0)
                slot(1, 1)
                with act.Fori(1, KM // 2 - 1) as i:
                    slot(i * 2, 0)
                    slot(i * 2 + 1, 1)
                slot(KM - 2, 0)
                slot(KM - 1, 1, last=True)

            def root_part(t, j):
                turn(2, root_mm)(t, j)
                hold("act", act, root_mm, t + 1)
                act.copy(root[:, bass.ds(t, 1), :], ps[:, j:j + 1, 0:D]).then_inc(root_out, 1)

            def neigh_part(t, j):
                turn(3, neigh_mm)(t, j)
                hold("act", act, pre_out, t + 1)
                act.activation(root[:, bass.ds(t, 1), :], root[:, bass.ds(t, 1), :], ACT.Relu).then_inc(h_out, 1)

            def squares(i):
                for b in range(2 * GBS[2]):
                    hold("act", act, gathered[2][b], (i + 1) * 16)
                    act.activation(gath[2][:, b, D:2 * D], gath[2][:, b, 0:D], ACT.Square).then_inc(squared, 1)

            std(1)
            pairs(act, rel_part)
            std(2)
            pairs(act, turn(1, routed))
            softmax_exp(1)
            experts(0)
            std(3)
            pairs(act, root_part)
            pairs(act, neigh_part)
            rounds(act, KS // (2 * GBS[2]), squares)
            act.wait_ge(gg_out, 1)
            act.activation(accx[:, :, 0:D], accx[:, :, 0:D], ACT.Tanh).then_inc(tanh_out, 1)
            std(4)
            pairs(act, turn(4, routed, base=T))
            softmax_exp(2)
            experts(1)

        @block.tensor
        def _(pe):
            pe.wait_ge(consts_in, 48)
            pe.wait_ge(set_pool, 1)

            def count(n, buckets):
                pe.wait_ge(ranked, n)
                pe.matmul(ps[:, 7, 0:buckets], below, cnt[:, 0, 0:buckets], start=True, stop=True)
                pe.matmul(ps[:, 7, 64:64 + buckets], ones[:, :], cnt[:, 0, 0:buckets], start=True, stop=True
                          ).then_inc(counted, 1)

            def turned_tiles(n, source, use):
                def turn(t):
                    if t >= 2:
                        pe.wait_ge(turned_in, n * T + t - 1)
                    for k in range(2):
                        last = pe.transpose(ps[:, 6 + t % 2, k * P:(k + 1) * P], source(t, k), ident)
                    last.then_inc(turned, 1)
                turn(0)
                for t in range(T):
                    if t + 1 < T:
                        turn(t + 1)
                    pe.wait_ge(turned_in, n * T + t + 1)
                    use(t, t % 2)

            def hn_half(t, k):
                return hn[:, t, k * P:(k + 1) * P]

            def rel_tile(t, j):
                for g in range(4):
                    if t:
                        pe.wait_ge(rel_act if g % 2 == 0 else rel_dve, 2 * (t - 1) + g // 2 + 1)
                    for k in range(2):
                        last = pe.matmul(ps[:, g, :], hT[:, j, k, :],
                                         w_rel[:, k, 2 * g:2 * g + 2, :].rearrange("p a b -> p (a b)"),
                                         start=(k == 0), stop=(k == 1))
                    last.then_inc(rel_mm, 1)

            def router_tile(l):
                def use(t, j):
                    for k in range(2):
                        last = pe.matmul(ps[:, 4, t * X:(t + 1) * X], hT[:, j, k, :], rw[:, l, k, :],
                                         start=(k == 0), stop=(k == 1))
                    last.then_inc(routed, 1)
                return use

            def root_tile(t, j):
                if t >= 2:
                    pe.wait_ge(root_out, t - 1)
                for k in range(2):
                    last = pe.matmul(ps[:, j, 0:D], hT[:, j, k, :], w_root[:, k, :], start=(k == 0), stop=(k == 1))
                last.then_inc(root_mm, 1)

            def neigh_tile(t, j):
                if t >= 2:
                    pe.wait_ge(pre_out, t - 1)
                for k in range(2):
                    last = pe.matmul(ps[:, 2 + j, 0:D], hT[:, j, k, :], w_neigh[:, k, :], start=(k == 0), stop=(k == 1))
                last.then_inc(neigh_mm, 1)

            def edge_sums(l):
                gb, w = GBS[l], width[l]

                def body(i):
                    for h in range(2):
                        hold("pe", pe, hot_out[l], i * 2 + (h + 1))
                        for b in range(h * gb, (h + 1) * gb):
                            hold("pe", pe, gathered[l][b], (i + 1) * 16)
                            if l == 2:
                                hold("pe", pe, squared, i * (2 * gb) + (b + 1))
                            k = i * (2 * gb) + b
                            if not isinstance(i, int) or k >= 8:
                                hold("pe", pe, added[l], k - 7)
                            pe.matmul(ps[:, b % 8, 0:w], hot[l][:, b, :], gath[l][:, b, 0:w],
                                      start=True, stop=True).then_inc(summed[l], 1)
                rounds(pe, KS // gb // 2, body)

            def experts(l):
                g = l * KM

                def xs_turn(k, j):
                    hold("pe", pe, xs_in[j], (k - j + 2 + g) * 8)
                    hold("pe", pe, xsT_in, k + g)
                    for c in range(2):
                        last = pe.transpose(ps[:, 5, c * P:(c + 1) * P], xs[:, j, c * P:(c + 1) * P], ident)
                    last.then_inc(xs_turned, 1)

                def hidden(k, j, e):
                    hold("pe", pe, xsT_in, k + (g + 1))
                    hold("pe", pe, hid_out, k + g)
                    if l == 0:
                        for w in range(2):
                            for b in range(2):
                                for c in range(2):
                                    last = pe.matmul(ps[:, 2 * w + b, 0:HH], xsT[:, j, c, :],
                                                     w13[:, 2 * w + c, bass.ds(e * H0 + b * HH, HH)],
                                                     start=(c == 0), stop=(c == 1))
                    else:
                        for c in range(2):
                            pe.matmul(ps[:, 0, 0:D], xsT[:, j, c, :], e1w1[:, c, bass.ds(e * D, D)],
                                      start=(c == 0), stop=False)
                        last = pe.matmul(ps[:, 0, 0:D], ones[0:1, :], e1b[:, 0, bass.ds(e * D, D)],
                                         start=False, stop=True)
                    last.then_inc(h_mm, 1)

                def results(k, j, e):
                    hold("pe", pe, hidT_act, k + (g + 1))
                    if l == 0:
                        hold("pe", pe, hidT_dve, k + 1)
                    hold("pe", pe, y_out, k + g)
                    if l == 0:
                        for c in range(NHC):
                            n = min(HC, H0 - c * HC)
                            last = pe.matmul(ps[:, 4, 0:D], hidT[0:n, j, c, :], w2[c][0:n, bass.ds(e * D, D)],
                                             start=(c == 0), stop=(c == NHC - 1))
                    else:
                        for c in range(2):
                            pe.matmul(ps[:, 4, 0:D], hidT[:, j, c, :], e1w2[:, c, bass.ds(e * D, D)],
                                      start=(c == 0), stop=False)
                        last = pe.matmul(ps[:, 4, 0:D], ones[0:1, :], e1b[:, 1, bass.ds(e * D, D)],
                                         start=False, stop=True)
                    last.then_inc(y_mm, 1)

                def hidden_turn(k):
                    hold("pe", pe, hid_out, k + (g + 1))
                    for c in range(NHC if l == 0 else 2):
                        n = min(HC, H0 - c * HC) if l == 0 else P
                        step = HC if l == 0 else P
                        last = pe.transpose(ps[0:n, 6 + c // 4, (c % 4) * P:(c % 4 + 1) * P],
                                            hid[:, c * step:c * step + n], ident)
                    last.then_inc(hid_turned, 1)

                def expert(k):
                    return pe.value_load(expert_of[0:1, bass.ds(k, 1)], min_val=0, max_val=X - 1)

                def slot(k, j, last=False):
                    hidden(k, j, expert(k))
                    if not isinstance(k, int) or k:
                        results(k - 1, 1 - j, expert(k - 1))
                    if not last:
                        xs_turn(k + 1, 1 - j)
                    hidden_turn(k)

                pe.wait_ge(tokens_placed, l + 1)
                if l == 0:
                    pe.wait_ge(w13_in, 64)
                    pe.wait_ge(w2_in, 16 * NHC)
                else:
                    pe.wait_ge(e1_in, 96)
                xs_turn(0, 0)
                slot(0, 0)
                slot(1, 1)
                with pe.Fori(1, KM // 2 - 1) as i:
                    slot(i * 2, 0)
                    slot(i * 2 + 1, 1)
                slot(KM - 2, 0)
                slot(KM - 1, 1, last=True)
                results(KM - 1, 1, expert(KM - 1))

            count(1, T)
            pe.wait_ge(w_rel_out, 1)
            pe.wait_ge(normed, T)
            turned_tiles(0, hn_half, rel_tile)
            count(2, T)
            edge_sums(0)
            pe.wait_ge(rw_in, 16)
            pe.wait_ge(normed, 2 * T)
            turned_tiles(1, hn_half, router_tile(0))
            count(3, X)
            experts(0)
            pe.wait_ge(normed, 3 * T)
            pe.wait_ge(wl_in, 32)
            turned_tiles(2, hn_half, root_tile)
            pe.wait_ge(root_out, T)
            edge_sums(1)
            pe.wait_ge(mean_out, 1)
            turned_tiles(3, lambda t, k: accx[:, t, k * P:(k + 1) * P], neigh_tile)
            edge_sums(2)
            pe.wait_ge(normed, 4 * T)
            turned_tiles(4, hn_half, router_tile(1))
            count(4, X)
            experts(1)

        @block.vector
        def _(dve):
            steps = [0]

            def then(ins):
                steps[0] += 1
                ins.then_inc(dve_step, 1)
                dve.wait_ge(dve_step, steps[0])

            def over_p(row, n):
                return row.unsqueeze(2).to_broadcast([row.shape[0], row.shape[1], n])

            def over_n(row, n):
                return row.unsqueeze(1).to_broadcast([row.shape[0], n, row.shape[1]])

            def rank_items(buckets, b, c, hots, scans, hots_flat, scans_flat, iota, result):
                then(dve.tensor_tensor(hots, over_n(buckets, b), over_p(iota, c), ALU.is_equal))
                then(dve.tensor_tensor_scan(scans_flat, hots_flat, hots_flat, 0.0, ALU.add, ALU.max))
                then(dve.tensor_copy(upto[:, 1:b + 1], scans[:, :, c - 1]))
                dve.tensor_tensor(cnt[:, 0, 0:b], upto[:, 1:b + 1], upto[:, 0:b], ALU.subtract).then_inc(ranked, 1)
                count_no[0] += 1
                dve.wait_ge(counted, count_no[0])
                then(dve.tensor_scalar(cnt_i[:, 0:b], ps[:, 7, 64:64 + b], float(P - 1), None, ALU.add))
                then(dve.tensor_scalar(cnt_i[:, 0:b], cnt_i[:, 0:b], 65535 - (P - 1), None, ALU.bitwise_and))
                then(dve.tensor_copy(cnt[:, 1, 0:b], cnt_i[:, 0:b]))
                then(dve.tensor_tensor_scan(cnt[:, 2, 0:b], cnt[:, 1, 0:b], cnt[:, 1, 0:b], 0.0, ALU.add, ALU.max))
                then(dve.tensor_tensor(cnt[:, 3, 0:b], cnt[:, 2, 0:b], cnt[:, 1, 0:b], ALU.subtract))
                then(dve.tensor_tensor(cnt[:, 3, 0:b], cnt[:, 3, 0:b], ps[:, 7, 0:b], ALU.add))
                then(dve.scalar_tensor_tensor(cnt[:, 3, 0:b], cnt[:, 3, 0:b], -1.0, upto[:, 0:b], ALU.add, ALU.subtract))
                then(dve.tensor_tensor(scans, scans, over_p(cnt[:, 3, 0:b], c), ALU.add))
                then(dve.tensor_tensor(scans, scans, hots, ALU.mult))
                then(dve.tensor_reduce(result, scans.rearrange("p b c -> p c b"), AX_X, ALU.add))

            count_no = [0]

            def slot_buckets(b, n, compare, result):
                ends = cnt[0:1, 2, 0:b]
                cmp = compare.rearrange("p (k b) -> p k b", b=b)
                then(dve.tensor_tensor(cmp, over_n(ends, n), over_p(starts[:, 0:n], b), ALU.is_le))
                then(dve.tensor_reduce(scan_row[:, 0:n], cmp, AX_X, ALU.add))
                then(dve.tensor_scalar(result, scan_row[:, 0:n], float(b - 1), None, ALU.min))

            scan_row = gloc[0:1, :]

            def read_edges():
                dve.wait_ge(edges_in, 48)
                src, dst, et = (raw[:, i, :] for i in range(3))
                for l, to in ((0, dst), (1, src)):
                    then(dve.tensor_scalar(work_i[:, 0, :], to, 7, None, ALU.logical_shift_right))
                    dve.tensor_copy(bucket[:, l, :], work_i[:, 0, :])
                    then(dve.tensor_scalar(work_i[:, 1 + l, :], to, P - 1, None, ALU.bitwise_and))
                then(dve.scalar_tensor_tensor(work_f[:, 0, :], src, float(NREL), et, ALU.mult, ALU.add))
                then(dve.scalar_tensor_tensor(load[:, 0, :], work_i[:, 1, :], float(PACK), work_f[:, 0, :],
                                              ALU.mult, ALU.add))
                then(dve.scalar_tensor_tensor(load[:, 1, :], work_i[:, 2, :], float(PACK), dst, ALU.mult, ALU.add))

            def sort_edges(l):
                rank_items(bucket[:, l, :], T, C, hot_sort, scan_sort, hot_flat, scan_flat, iota_t, sort_f[:, 0, :])
                then(dve.tensor_copy(sort_i[:, 0, :], sort_f[:, 0, :]))
                then(dve.tensor_scalar(sort_i[:, 1, :], sort_i[:, 0, :], P - 1, None, ALU.bitwise_and))
                then(dve.tensor_scalar(sort_i[:, 0, :], sort_i[:, 0, :], 7, None, ALU.logical_shift_right))
                then(dve.scalar_tensor_tensor(sort_f[:, 0, :], sort_i[:, 1, :], float(KS), sort_i[:, 0, :],
                                              ALU.mult, ALU.add))
                then(dve.tensor_scalar(sort_f[:, 1, :], bucket[:, l, :], float(T), SKIP, ALU.is_ge, ALU.mult))
                then(dve.tensor_tensor(place[:, l, :], sort_f[:, 0, :], sort_f[:, 1, :], ALU.add))
                slot_buckets(T, KS, at(0, KS * T, parts=1), block_of[:, l, :])
                dve.sem_inc(edges_placed, 1)

            sort_f = at(0, 2, C)
            sort_i = at(2 * C, 2, C, dt=I32)

            def relation_weights():
                dve.wait_ge(wc_in, 16 * NREL)
                for k in range(2):
                    dve.wait_ge(basis_in[k], 16 * NREL)
                    then(dve.tensor_scalar(w_rel[:, k, :, :], basis_sb[:, :, 0, :], wc[:, 0:1], None, ALU.mult))
                    for b in range(1, NBASES):
                        then(dve.scalar_tensor_tensor(w_rel[:, k, :, :], basis_sb[:, :, b, :], wc[:, b:b + 1],
                                                      w_rel[:, k, :, :], ALU.mult, ALU.add))
                    dve.sem_inc(basis_used if k == 0 else w_rel_out, 1)

            def layer_norm(n):
                U = 5
                with dve.Fori(0, T // U) as i:
                    for u in range(U):
                        t = i * U + u
                        dve.bn_stats(stats[:, bass.ds(t, 1), :].rearrange("p a b -> p (a b)"),
                                     x[:, bass.ds(t, 1), :].rearrange("p a b -> p (a b)")).then_inc(stat_out, 1)
                dve.wait_ge(stat_out, n * T)
                then(dve.tensor_tensor(mean[:, :], stats[:, :, 1], stats[:, :, 4], ALU.add))
                then(dve.tensor_tensor(rstd[:, :], stats[:, :, 1], stats[:, :, 4], ALU.subtract))
                then(dve.tensor_tensor(rstd[:, :], rstd[:, :], rstd[:, :], ALU.mult))
                then(dve.tensor_scalar(rstd[:, :], rstd[:, :], 0.25, EPS, ALU.mult, ALU.add))
                then(dve.tensor_tensor(stats[:, :, 2], stats[:, :, 2], stats[:, :, 5], ALU.add))
                then(dve.scalar_tensor_tensor(rstd[:, :], stats[:, :, 2], 1.0 / D, rstd[:, :], ALU.mult, ALU.add))
                dve.tensor_scalar(mean[:, :], mean[:, :], 0.5, None, ALU.mult).then_inc(var_out, 1)
                dve.wait_ge(std_out, n)
                then(dve.reciprocal(rstd[:, :], rstd[:, :]))
                with dve.Fori(0, T // U) as i:
                    for u in range(U):
                        t = bass.ds(i * U + u, 1)
                        dve.tensor_scalar(hn[:, t, :], x[:, t, :], mean[:, t], rstd[:, t],
                                          ALU.subtract, ALU.mult).then_inc(normed, 1)

            def rel_part(t, j):
                hold("dve", dve, rel_stored[j], (t - j) * 8)
                for g in (1, 3):
                    hold("dve", dve, rel_mm, t * 4 + g + 1)
                    dve.tensor_copy(rel_out[:, j, g * 512:(g + 1) * 512], ps[:, g, :]).then_inc(rel_dve, 1)

            def unpack(l):
                dve.wait_ge(list_in, 16 * (l + 1))
                dve.tensor_scalar(gidx[:, :], packed, PACK - 1, None, ALU.bitwise_and)
                then(dve.tensor_scalar(gloc_i, packed, 15, None, ALU.logical_shift_right))
                then(dve.tensor_copy(gloc[:, :], gloc_i))
                dve.sem_inc(list_ready, 1)

            def edge_sums(l):
                gb, w, lst = GBS[l], width[l], min(l, 1)

                def one_hot(i, h):
                    if not isinstance(i, int):
                        hold("dve", dve, summed[l], i * (2 * gb) + (h - 1) * gb)
                    nodes = gloc[:, bass.ds((i * 2 + h) * gb, gb)]
                    dve.tensor_tensor(hot[l][:, h * gb:(h + 1) * gb, :], over_n(lane, gb), over_p(nodes, P),
                                      ALU.is_equal).then_inc(hot_out[l], 1)

                def add(i, h):
                    for b in range(h * gb, (h + 1) * gb):
                        k = i * (2 * gb) + b
                        blk = dve.value_load(block_of[0:1, lst, bass.ds(k, 1)], min_val=0, max_val=T - 1)
                        hold("dve", dve, summed[l], k + 1)
                        hold("dve", dve, added[l], k)
                        to = acc[l][:, bass.ds(blk, 1), 0:w]
                        dve.tensor_tensor(to, to, ps[:, b % 8:b % 8 + 1, 0:w], ALU.add).then_inc(added[l], 1)

                def body(i):
                    one_hot(i, 0)
                    if not isinstance(i, int):
                        add(i - 1, 1)
                    one_hot(i, 1)
                    add(i, 0)
                n = KS // gb // 2
                rounds(dve, n, body)
                add(n - 1, 1)
                dve.wait_ge(added[l], KS)

            def route(l):
                flat = [lg[:, i, :, :] for i in range(4)]
                dve.wait_ge(routed, (l + 1) * T)
                then(dve.tensor_copy(flat[0].rearrange("p a b -> p (a b)"), ps[:, 4, 0:T * X]))
                then(dve.tensor_reduce(tops[:, 0, :], flat[0], AX_X, ALU.max))
                dve.tensor_tensor(flat[1], flat[0], over_p(tops[:, 0, :], X), ALU.subtract).then_inc(lgm_out, 1)
                dve.wait_ge(exp_out, l + 1)
                then(dve.tensor_reduce(tops[:, 0, :], flat[1], AX_X, ALU.add))
                then(dve.reciprocal(tops[:, 0, :], tops[:, 0, :]))
                then(dve.tensor_tensor(flat[1], flat[1], over_p(tops[:, 0, :], X), ALU.mult))
                for c in range(TOPK):
                    then(dve.tensor_reduce(gates[:, c, :], flat[1], AX_X, ALU.max))
                    then(dve.tensor_tensor(flat[2], flat[1], over_p(gates[:, c, :], X), ALU.is_equal))
                    then(dve.scalar_tensor_tensor(flat[2], flat[2], -float(X), over_n(iota_x8, T), ALU.mult, ALU.add))
                    then(dve.tensor_reduce(choice[:, c, :], flat[2], AX_X, ALU.min))
                    if c + 1 < TOPK:
                        then(dve.tensor_tensor(flat[2], over_n(iota_x, T), over_p(choice[:, c, :], X), ALU.is_equal))
                        then(dve.scalar_tensor_tensor(flat[1], flat[2], -2.0, flat[1], ALU.mult, ALU.add))
                then(dve.tensor_tensor(tops[:, 1, :], gates[:, 0, :], gates[:, 1, :], ALU.add))
                if l == 0:
                    then(dve.tensor_scalar(tops[:, 1, :], tops[:, 1, :], 1e-9, None, ALU.add))
                else:
                    then(dve.tensor_scalar(tops[:, 1, :], tops[:, 1, :], 1e-12, None, ALU.max))
                then(dve.reciprocal(tops[:, 1, :], tops[:, 1, :]))
                then(dve.tensor_tensor(gates[:, :, :], gates[:, :, :], over_n(tops[:, 1, :], TOPK), ALU.mult))
                then(dve.tensor_tensor(choice[:, :, :], choice[:, :, :], over_n(beyond, TOPK), ALU.add))
                ch = choice[:, :, :].rearrange("p a b -> p (a b)")
                m0, m1 = (msort[:, i, :, :] for i in range(2))
                rank_items(ch, X, CM, m0, m1, m0.rearrange("p a b -> p (a b)"), m1.rearrange("p a b -> p (a b)"),
                           iota_x, rank[:, :])
                then(dve.tensor_scalar(tplace[:, 1, :], rank[:, :], 0.0, None, ALU.max))
                then(dve.tensor_scalar(ch, ch, float(X), SKIP, ALU.is_ge, ALU.mult))
                then(dve.tensor_tensor(tplace[:, 0, :], rank[:, :], ch, ALU.add))
                cm2 = msort[0:1, :, :, :].rearrange("p j a b -> p (j a b)")[:, 0:KM * X]
                slot_buckets(X, KM, cm2, expert_of[:, :])
                dve.sem_inc(tokens_placed, 1)

            def experts(l):
                g = l * KM

                def slot(k, j, first=False):
                    if l == 0:
                        hold("dve", dve, act_out, k + 1)
                        dve.tensor_tensor(hid.rearrange("p (b h) -> p b h", b=2), hid.rearrange("p (b h) -> p b h", b=2),
                                          ps[:, 2:4, 0:HH], ALU.mult).then_inc(hid_out, 1)
                    if not first:
                        result(k - 1, 1 - j)
                    if l == 0:
                        hold("dve", dve, hid_turned, k + 1)
                        hold("dve", dve, y_mm, k - 1)
                        dve.tensor_copy(hidT[0:HC, j, 4:NHC, :],
                                        ps[0:HC, 7, 0:(NHC - 4) * P].rearrange("p (k d) -> p k d", k=NHC - 4)
                                        ).then_inc(hidT_dve, 1)

                def result(k, j):
                    hold("dve", dve, y_mm, k + (g + 1))
                    hold("dve", dve, ys_stored[j], (k - j + g) * 8)
                    dve.tensor_copy(ys[:, j, :], ps[:, 4, 0:D]).then_inc(y_out, 1)
                slot(0, 0, first=True)
                slot(1, 1)
                with dve.Fori(1, KM // 2) as i:
                    slot(i * 2, 0)
                    slot(i * 2 + 1, 1)
                result(KM - 1, 1)

            def combine(l):
                for c in range(CM):
                    if c % BG == 0:
                        dve.wait_ge(back[c // BG], 16 * BG * (l + 1))
                    if c >= T:
                        dve.wait_ge(combined, l * CM + c - T + 1)
                    t = c % T
                    dve.scalar_tensor_tensor(x[:, t, :], y_back[:, c, :], gates[:, c // T, t:t + 1], x[:, t, :],
                                             ALU.mult, ALU.add).then_inc(combined, 1)
                dve.wait_ge(combined, (l + 1) * CM)
                dve.sem_inc(combined_all, 1)

            dve.wait_ge(consts_in, 48)
            then(dve.memset(upto[:, :], 0.0))
            read_edges()
            sort_edges(0)
            dve.wait_ge(x_in, 32)
            dve.wait_ge(tok_init, 16 * KM // 8)
            layer_norm(1)
            relation_weights()
            pairs(dve, rel_part)
            sort_edges(1)
            dve.wait_ge(turned_in, T)
            then(dve.memset(acc0[:, :, :], 0.0))
            unpack(0)
            edge_sums(0)
            dve.wait_ge(bias_in, 32)
            then(dve.tensor_tensor(acc0[:, :, :], acc0[:, :, :], over_n(bias0[:, :], T), ALU.add))
            then(dve.scalar_tensor_tensor(x[:, :, :], acc0[:, :, :], 0.0, x[:, :, :], ALU.max, ALU.add))
            layer_norm(2)
            route(0)
            experts(0)
            combine(0)
            layer_norm(3)
            then(dve.memset(accx, 0.0))
            then(dve.memset(acch, 0.0))
            then(dve.memset(gath[1][:, :, D:D + 1], 1.0))
            unpack(1)
            edge_sums(1)
            then(dve.tensor_copy(deg[:, 0, :], accx[:, :, D]))
            then(dve.tensor_scalar(deg[:, 1, :], deg[:, 0, :], 1.0, None, ALU.max))
            then(dve.reciprocal(deg[:, 1, :], deg[:, 1, :]))
            dve.tensor_tensor(accx[:, :, 0:D], accx[:, :, 0:D], over_p(deg[:, 1, :], D), ALU.mult).then_inc(mean_out, 1)
            dve.wait_ge(root_out, T)
            then(dve.tensor_tensor(root, root, over_n(bias1[:, :], T), ALU.add))

            def neigh_part(t, j):
                hold("dve", dve, neigh_mm, t + 1)
                r = root[:, bass.ds(t, 1), :]
                dve.tensor_tensor(r, r, ps[:, 2 + j:3 + j, 0:D], ALU.add).then_inc(pre_out, 1)
            pairs(dve, neigh_part)
            edge_sums(2)
            g = accx[:, :, 0:D]
            dve.wait_ge(h_out, T)
            dve.wait_ge(h_stored, 16)
            then(dve.tensor_tensor(g, root, over_p(deg[:, 0, :], D), ALU.mult))
            then(dve.scalar_tensor_tensor(g, acch[:, :, 0:D], -2.0, g, ALU.mult, ALU.add))
            then(dve.tensor_tensor(g, g, root, ALU.mult))
            then(dve.tensor_tensor(g, g, acch[:, :, D:2 * D], ALU.add))
            dve.tensor_tensor(g, g, over_p(deg[:, 1, :], D), ALU.mult).then_inc(gg_out, 1)
            dve.wait_ge(tanh_out, 1)
            then(dve.tensor_tensor(x[:, :, :], x[:, :, :], g, ALU.add))
            dve.sem_inc(graph_done, 1)
            layer_norm(4)
            dve.wait_ge(normed, 4 * T)
            then(dve.tensor_tensor(x[:, :, :], x[:, :, :], hn[:, :, :], ALU.add))
            route(1)
            experts(1)
            combine(1)


def kernel(**inputs):
    import numpy as np
    import concourse.bacc as bacc
    from concourse.bass_utils import run_bass_kernel_spmd as run

    def c(name):
        return np.ascontiguousarray(inputs[name])

    def edges(name, fill):
        v = np.full(P * C, fill, np.int32)
        v[:E] = inputs[name]
        return v.reshape(P, C)

    i = np.arange(P)
    tiles = np.arange(T)
    small = np.concatenate([
        np.broadcast_to(tiles, (P, T)), np.broadcast_to(np.arange(X), (P, X)), np.broadcast_to(np.arange(X) + X, (P, X)),
        np.where(tiles[None, :] * P + i[:, None] >= N, 100, 0)], 1).astype(np.float32)
    rw = np.stack([c("L0_ffn_router_w"), c("L1_ffn_router_w")])
    arrays = {
        "x": c("x"), "src": edges("src", NP), "dst": edges("dst", NP), "et": edges("edge_type_8", 0),
        "c_mats": np.concatenate([np.eye(P), i[:, None] < i[None, :], np.broadcast_to(i, (P, P))], 1).astype(np.float32),
        "c_small": small, "c_starts": (np.arange(KS, dtype=np.float32) * P)[None],
        "basis": c("L0_gnn_basis").reshape(NBASES * D, D), "w_comp": c("L0_gnn_w_comp"),
        "bias0": c("L0_gnn_bias").reshape(1, D), "bias1": c("L1_gnn_b").reshape(1, D),
        "rw": np.ascontiguousarray(rw.reshape(2, X, 2, P).transpose(3, 0, 2, 1)),
        "w1": np.ascontiguousarray(c("L0_ffn_w1").transpose(0, 2, 1)),
        "w3": np.ascontiguousarray(c("L0_ffn_w3").transpose(0, 2, 1)),
        "w2": np.ascontiguousarray(c("L0_ffn_w2").transpose(0, 2, 1)),
        "W_root": c("L1_gnn_W_root"), "W_neigh": c("L1_gnn_W_neigh"),
        "e1w1": c("L1_ffn_w1"), "e1b1": c("L1_ffn_b1").reshape(1, X * D),
        "e1w2": c("L1_ffn_w2"), "e1b2": c("L1_ffn_b2").reshape(1, X * D),
    }
    nc = bacc.Bacc("TRN2", target_bir_lowering=False, num_devices=1)
    aps = {n: nc.dram_tensor("in_" + n, v.shape, mybir.dt.from_np(v.dtype), kind="ExternalInput").ap()
           for n, v in arrays.items()}
    out = nc.dram_tensor("out", (N, D), F32, kind="ExternalOutput").ap()
    program(nc, aps, out)
    r = run(nc, [{"in_" + n: v for n, v in arrays.items()}], core_ids=[0])
    return r.results[0]["out"]
```

```python
from contextlib import ExitStack

import concourse.bass as bass
from concourse import mybir

F32 = mybir.dt.float32
F16 = mybir.dt.float16
I32 = mybir.dt.int32
ALU = mybir.AluOpType
ACT = mybir.ActivationFunctionType
AX_X = mybir.AxisListType.X

P = 128
N, D = 3125, 256
T = -(-N // P)
NP = T * P
E = 50000
C = 392
NREL, NBASES = 8, 4
KS = 416
X, TOPK = 8, 2
H0 = 682
HH = H0 // 2
HC = 114
NHC = -(-H0 // HC)
CM = TOPK * T
KM = 56
EPS = 1e-5
SKIP = 1.0e6
PACK = 32768
SB = 14
C_SCAT = (224, C)
PB = 4
HALF_BITS = 11
COUNT_1, COUNT_2 = 3, 12
PERM_FROM = 17
GB = 8
BPW = 4
PARTS = (0, 5, 10, 15, 20, KS // (2 * GB))
ST = 5
TG = 5
XB = 4
SCAT_EARLY = 4
assert C * P >= E and all(c % (2 * SB) == 0 and (C - c) % (2 * PB) == 0 for c in C_SCAT) and KS % (2 * GB) == 0 and GB % BPW == 0
assert KS >= (E + T * (P - 1)) // P and KM >= (N * TOPK + X * (P - 1)) // P and T % 2 and KM % 2 == 0
assert C_SCAT[1] == SCAT_EARLY * 2 * SB + ST * KM and SB >= 2 * ST and T == (len(PARTS) - 1) * TG
assert T ** BPW < 1 << 24 and P * PACK + N * NREL < 1 << 24 and NP * NREL <= PACK


def program(nc, a, out):
    rel_table = nc.dram_tensor("rel_table", [NP * NREL, D], F32)
    hn_tables = [nc.dram_tensor(f"hn_table{i}", [NP, D], F32) for i in range(3)]
    h_table = nc.dram_tensor("h_table", [NP, D], F32)
    sorted_edges = [nc.dram_tensor(f"sorted_edges{l}", [P * KS, 1], I32) for l in range(2)]
    results = nc.dram_tensor("results", [CM * P, D], F32)

    with ExitStack() as ctx:
        def sb(name, shape, dt=F32):
            return ctx.enter_context(nc.sbuf_tensor(name, shape, dt))

        def sem(name):
            return ctx.enter_context(nc.semaphore(name))

        x = sb("x", [P, T, D])
        hn = sb("hn", [P, T, D])
        consts = sb("consts", [P, 3 * P])
        ident, below, lane = (consts[:, i * P:(i + 1) * P] for i in range(3))
        ones = sb("ones", [P, P])
        small = sb("small", [P, T + 2 * X + T + CM])
        choice_id = small[:, 2 * T + 2 * X:]
        iota_t, iota_x, iota_x8 = small[:, 0:T], small[:, T:T + X], small[:, T + X:T + 2 * X]
        beyond = small[:, T + 2 * X:2 * T + 2 * X]
        starts = sb("starts", [P, 2 * KM + BPW])
        tok_starts, word_starts = starts[0:1, 0:KM], starts[:, KM:KM + BPW]
        slot_no = starts[:, KM + BPW:]
        slot_word = sb("slot_word", [P, 2, BPW])
        slot_word_i = sb("slot_word_i", [P, 2], I32)
        bias0 = sb("bias0", [P, D])
        rw = sb("rw", [P, 2, 2, X])
        wc = sb("wc", [P, NBASES])
        gidx = sb("gidx", [P, KS], I32)
        lists = sb("lists", [P, 2 * KS], I32)
        packed, gloc_i = lists[:, 0:KS], lists[:, KS:2 * KS]
        lg = lists[:, 0:4 * T * X].bitcast(F32).rearrange("p (i t e) -> p i t e", i=4, t=T)
        gloc = sb("gloc", [P, KS])
        sort_work = sb("sort_work", [P, 2 * X * CM])
        bucket = sort_work[:, 0:2 * C].rearrange("p (l c) -> p l c", l=2)
        msort = sort_work[:, :].rearrange("p (i e c) -> p i e c", i=2, e=X)
        place = sb("place", [P, 2, C], I32)
        load = sb("load", [P, 2, C], I32)
        block_of = sb("block_of", [1, 2, KS // BPW], I32)
        expert_of = sb("expert_of", [1, KM], I32)
        stg_place = sb("stg_place", [P, 2, SB], I32)
        stg_load = sb("stg_load", [P, 2, SB], I32)
        stg_g = sb("stg_g", [P, 2, GB], I32)
        stats = sb("stats", [P, T, 6])
        mean = sb("mean", [P, T])
        rstd = sb("rstd", [P, T])
        upto = sb("upto", [P, T + 1])
        cnt = sb("cnt", [P, 4, T])
        cnt_i = sb("cnt_i", [P, T], I32)
        hT = sb("hT", [P, 2, 2, P])
        gates = sb("gates", [P, TOPK, T])
        tops = sb("tops", [P, 2, T])
        choice = sb("choice", [P, TOPK, T])
        rank = sb("rank", [P, CM])
        place_i = sb("place_i", [P, 2, CM], I32)
        place_f = sb("place_f", [P, 2, CM])
        tok_rows = sb("tok_rows", [P, KM + XB, 2], I32)
        stg_tok = sb("stg_tok", [P, XB, 2], I32)
        slot_tok = sb("slot_tok", [P, 3, KM])
        deg = sb("deg", [P, 2, T])

        ARENA = 4 * X * H0 + (NHC - 1) * X * D
        arena = sb("arena", [P, ARENA])

        def at(off, *shape, dt=F32, parts=P):
            n = 1
            for d in shape:
                n *= d
            n = n // 2 if dt == F16 else n
            assert off + n <= ARENA
            v = arena[0:parts, off:off + n]
            if dt != F32:
                v = v.bitcast(dt)
            names = "abc"[:len(shape)]
            if len(shape) > 1:
                v = v.rearrange(f"p ({' '.join(names)}) -> p {' '.join(names)}", **dict(zip(names[:-1], shape)))
            return v

        hot_sort, scan_sort = at(0, T, C, dt=F16), at(T * C, T, C)
        hot_flat, scan_flat = at(0, T * C, dt=F16), at(T * C, T * C)
        basis_sb = [at(k * T * C, NREL, NBASES, D) for k in range(2)]
        w_rel = at(2 * T * C, 2, NREL, D)
        o = 2 * T * C + 2 * NREL * D
        rel_out = at(o, 2, NREL * D)
        raw = at(o, 3, C, dt=I32)
        work_i = at(o + 3 * C, 3, C, dt=I32)
        work_f = at(o + 6 * C, 2, C)
        o += 2 * NREL * D
        perm_row = at(o, 2 * PB, 2, P, dt=F16)
        perm_col = at(o + 2 * PB * P, 2 * PB, KS, dt=F16)
        o += 2 * PB * P + PB * KS
        count_h = at(o, KS + P, dt=F16)
        count_cols, count_rows = count_h[:, 0:KS], count_h[:, KS:KS + P]
        o += (KS + P) // 2
        CP = C - C_SCAT[0]
        row_of, col_of, part_a, part_b = (at(o + i * CP, CP) for i in range(4))
        part_i = at(o + 4 * CP, CP, dt=I32)
        w13 = at(0, 4, X * H0)
        o = 4 * X * H0
        gath = [[at(o + b * D, D) for b in range(2 * GB)]]
        hot = [at(o + 2 * GB * D, 2 * GB, P)]
        w2a = at(o, NHC - 1, X * D)
        acc0 = hn
        hnf = hn[:, :, :].rearrange("p a b -> p (a b)")
        xs = hnf[:, 0:XB * D].rearrange("p (j d) -> p j d", j=XB)
        o = XB * D
        xsT = hnf[:, o:o + 512].rearrange("p (j k d) -> p j k d", j=2, k=2)
        ys = hnf[:, o + 512:o + 1024].rearrange("p (j d) -> p j d", j=2)
        hid = hnf[:, o + 1024:o + 1024 + H0]
        o += 1024 + H0
        hidT = hnf[:, o:o + 2 * NHC * P].rearrange("p (j k d) -> p j k d", j=2, k=NHC)
        o += 2 * NHC * P
        w2b = hnf[:, o:o + X * D]
        w2 = [w2a[:, k, :] for k in range(NHC - 1)] + [w2b]
        y_back = at(0, CM, D)
        hot_rows = [at(o, CM, P) for o in (4 * X * H0, 0)]
        hot_cols = [at(o + CM * P, CM, KM) for o in (4 * X * H0, 0)]
        root = at(0, T, D)
        accx = at(T * D, T, D + 1)
        o = T * (2 * D + 1)
        acch = at(o, T, 2 * D)
        o += T * 2 * D
        g1 = at(T * (2 * D + 1), 2 * GB, D + 1)
        gath.append([g1[:, b, :] for b in range(2 * GB)])
        hot.append(at(T * (2 * D + 1) + 2 * GB * (D + 1), 2 * GB, P))
        gath.append([at(o + b * 2 * D, 2 * D) for b in range(GB)] +
                    [hnf[:, b * 2 * D:(b + 1) * 2 * D] for b in range(GB)])
        hot.append(hnf[:, GB * 2 * D:GB * (2 * D + 2 * P)].rearrange("p (b n) -> p b n", n=P))
        o += 2 * GB * D
        w_root, w_neigh, bias1 = at(o, 2, D), at(o + 2 * D, 2, D), at(o + 4 * D, D, parts=1)
        e1w1, e1w2 = at(CM * D, 2, X * D), at(CM * D + 2 * X * D, 2, X * D)
        e1b = at(CM * D + 4 * X * D, 2, X * D, parts=1)
        acc = [acc0[:, :, :], accx, acch]
        width = [D, D + 1, 2 * D]

        ps = ctx.enter_context(nc.psum_tensor("ps", [P, 8, 512], F32))

        edges_in, consts_in, x_in, wc_in, bias_in, rw_in = map(
            sem, "edges_in consts_in x_in wc_in bias_in rw_in".split())
        basis_in = [sem("basis_in0"), sem("basis_in1")]
        set_pool, pad_set, zero_set, lists_init = map(
            sem, "set_pool pad_set zero_set lists_init".split())
        dve_step, ranked, counted, edges_placed, tokens_placed = map(
            sem, "dve_step ranked counted edges_placed tokens_placed".split())
        staged, list_in, list_ready = map(sem, "staged list_in list_ready".split())
        word_out, words_in, perm_out, permuted = map(sem, "word_out words_in perm_out permuted".split())
        scattered = [sem("scattered0"), sem("scattered1")]
        stat_out = sem("stat_out")
        var_out, std_out, normed, turned, turned_in, routed = map(
            sem, "var_out std_out normed turned turned_in routed".split())
        w_rel_out, rel_mm, rel_copied = map(sem, "w_rel_out rel_mm rel_copied".split())
        rel_stored = [sem("rel_stored0"), sem("rel_stored1")]
        gathered = [[sem(f"gathered{l}_{b}") for b in range(2 * GB)] for l in range(3)]
        hot_out = [sem(f"hot_out{l}") for l in range(3)]
        summed = [sem(f"summed{l}") for l in range(3)]
        added = [sem(f"added{l}") for l in range(3)]
        staged_g = [sem(f"staged_g{l}") for l in range(3)]
        squared, begun = sem("squared"), sem("begun")
        w13_in, w2_in, e1_in, wl_in = map(sem, "w13_in w2_in e1_in wl_in".split())
        lgm_out, exp_out, hots_out, tok_permuted, tok_staged = map(
            sem, "lgm_out exp_out hots_out tok_permuted tok_staged".split())
        hn_stored = [sem(f"hn_stored{i}") for i in range(3)]
        xs_in = [sem(f"xs_in{j}") for j in range(XB)]
        xs_turned, xsT_in, h_mm, act_out, hid_out, hid_turned, hidT_act, hidT_dve, y_mm, y_out = map(
            sem, "xs_turned xsT_in h_mm act_out hid_out hid_turned hidT_act hidT_dve y_mm y_out".split())
        ys_stored = [sem("ys_stored0"), sem("ys_stored1")]
        back = [sem(f"back{g}") for g in range(CM // TG)]
        combined, combined_all, root_mm, root_out, neigh_mm, pre_out, h_out, h_stored = map(
            sem, "combined combined_all root_mm root_out neigh_mm pre_out h_out h_stored".split())
        gg_out, tanh_out, tanh_added, graph_done, out_stored = map(
            sem, "gg_out tanh_out tanh_added graph_done out_stored".split())
        passed = {e: sem(f"passed_{e}") for e in ("sp", "pool", "act", "dve", "pe")}

        def hold(e, eng, semaphore, value):
            if isinstance(value, int):
                if value > 0:
                    eng.wait_ge(semaphore, value)
            else:
                eng.wait_ge(semaphore, value)
                eng.sem_inc(passed[e], 1)

        def pairs(eng, body):
            for t in range(3):
                body(t, t % 2)
            with eng.Fori(1, T // 2) as i:
                body(i * 2 + 1, 1)
                body(i * 2 + 2, 0)

        def rounds(eng, n, body, first=0):
            if first == 0:
                body(0)
            with eng.Fori(max(first, 1), n) as i:
                body(i)

        block = ctx.enter_context(nc.Block())

        @block.sync
        def _(sp):
            full = (T - 1) * P
            for i, name in enumerate(("src", "dst", "et")):
                sp.dma_start(raw[:, i, :], a[name]).then_inc(edges_in, 16)
            sp.dma_start(consts[:, :], a["c_mats"]).then_inc(consts_in, 16)
            sp.dma_start(small[:, :], a["c_small"]).then_inc(consts_in, 16)
            sp.dma_start(starts[:, :], a["c_starts"]).then_inc(consts_in, 16)
            sp.dma_start(count_h, a["c_count"]).then_inc(consts_in, 16)
            sp.wait_ge(zero_set, 1)
            sp.dma_start(x[:, 0:T - 1, :], a["x"][0:full, :].rearrange("(t p) d -> p t d", p=P)
                         ).then_inc(x_in, 16)
            sp.dma_start(x[0:N - full, T - 1, :], a["x"][full:N, :]).then_inc(x_in, 16)
            for r in range(NREL):
                sp.dma_start(wc[r::NREL, :], a["w_comp"][r:r + 1, :].to_broadcast([P // NREL, NBASES])
                             ).then_inc(wc_in, 16)
            sp.dma_start(bias0[:, :], a["bias0"].to_broadcast([P, D])).then_inc(bias_in, 16)
            sp.dma_start(rw[:, :, :, :], a["rw"]).then_inc(rw_in, 16)
            bases = a["basis"].rearrange("(s q b) o -> q s (b o)", q=P // 4, b=NBASES)
            for k in range(2):
                for r in range(NREL):
                    sp.dma_start(basis_sb[k][r::NREL, :, :, :].rearrange("p a b c -> p a (b c)"),
                                 bases[k * P // NREL:(k + 1) * P // NREL]).then_inc(basis_in[k], 16)
            sp.wait_ge(pad_set, 2)
            for l, pad in ((0, packed), (1, gloc_i)):
                sp.dma_start(sorted_edges[l][:, :].rearrange("(p k) o -> p (k o)", p=P), pad
                             ).then_inc(lists_init, 16)
            def store_rel(t, j):
                hold("sp", sp, rel_copied, t * 4 + 4)
                sp.dma_start(rel_table[bass.ds(t * (P * NREL), P * NREL), :].rearrange("(p r) d -> p (r d)", r=NREL),
                             rel_out[:, j, :]).then_inc(rel_stored[j], 16)
            pairs(sp, store_rel)
            for l in range(2):
                sp.wait_ge(word_out, l + 1)
                sp.dma_start(block_of[0:1, l, :], slot_word_i[0:KS // BPW, l:l + 1]).then_inc(words_in, 16)

            def load_list(l):
                for h in range(2):
                    sp.wait_ge(scattered[h], 16 * sum(C_SCAT[0:l + 1]) // 2)
                sp.dma_start(packed, sorted_edges[l][:, :].rearrange("(p k) o -> p (k o)", p=P)
                             ).then_inc(list_in, 16)
            load_list(0)
            sp.wait_ge(permuted, CP)
            sp.wait_ge(edges_placed, 2)
            sp.wait_ge(rel_mm, 4 * T)
            for e in range(X):
                sp.wait_ge(added[0], (e + 1) * (KS // 2 // X))
                for i, name in enumerate(("w1", "w1", "w3", "w3")):
                    sp.dma_start(w13[:, i, e * H0:(e + 1) * H0], a[name][e, (i % 2) * P:(i % 2 + 1) * P, :]
                                 ).then_inc(w13_in, 16)


            def store_table(table, rows, ready, past, stored):
                for t in range(0, T, TG):
                    sp.wait_ge(ready, past + t + TG)
                    sp.dma_start(table[t * P:(t + TG) * P, :].rearrange("(t p) d -> p t d", p=P),
                                 rows[:, t:t + TG, :]).then_inc(stored, 16)

            def load_results(l):
                for j in range(2):
                    sp.wait_ge(ys_stored[j], 16 * (KM // 2) * (l + 1))
                for c in range(0, CM, TG):
                    whole = TG - 1 if (c + TG) % T == 0 else TG
                    sp.dma_start(y_back[:, c:c + whole, :], results[c * P:(c + whole) * P, :].rearrange("(t p) d -> p t d", p=P)
                                 ).then_inc(back[c // TG], 16)
                    if whole < TG:
                        at_ = (c + whole) * P
                        sp.dma_start(y_back[0:N - full, c + whole, :], results[at_:at_ + N - full, :]
                                     ).then_inc(back[c // TG], 16)

            store_table(hn_tables[0], hn, normed, T, hn_stored[0])
            sp.wait_ge(tok_permuted, 1)
            for k in range(NHC):
                n = min(HC, H0 - k * HC)
                if k == NHC - 1:
                    sp.wait_ge(tokens_placed, 1)
                    sp.wait_ge(hn_stored[0], 16 * T // TG)
                sp.dma_start(w2[k][0:n, :].rearrange("p (e d) -> p e d", e=X),
                             a["w2"][:, k * HC:k * HC + n, :].rearrange("e h d -> h e d")).then_inc(w2_in, 16)
            load_list(1)
            load_results(0)
            sp.wait_ge(combined_all, 1)
            for name, w in (("W_root", w_root), ("W_neigh", w_neigh)):
                sp.dma_start(w, a[name].rearrange("(k p) d -> p k d", p=P)).then_inc(wl_in, 16)
            sp.dma_start(bias1, a["bias1"]).then_inc(wl_in, 16)
            store_table(hn_tables[1], hn, normed, 2 * T, hn_stored[1])
            store_table(h_table, root, h_out, 0, h_stored)
            sp.wait_ge(graph_done, 1)
            for k in range(2):
                for name, w in (("e1w1", e1w1), ("e1w2", e1w2)):
                    sp.dma_start(w[:, k, :].rearrange("p (e h) -> p e h", e=X),
                                 a[name][:, k * P:(k + 1) * P, :].rearrange("e c h -> c e h")).then_inc(e1_in, 16)
                sp.dma_start(e1b[:, k, :], a[f"e1b{k + 1}"]).then_inc(e1_in, 16)
            store_table(hn_tables[2], hn, normed, 3 * T, hn_stored[2])
            load_results(1)
            sp.wait_ge(combined_all, 2)
            sp.dma_start(out[0:full, :].rearrange("(t p) d -> p t d", p=P), x[:, 0:T - 1, :]).then_inc(out_stored, 16)
            sp.dma_start(out[full:N, :], x[0:N - full, T - 1, :]).then_inc(out_stored, 16)
            sp.wait_ge(out_stored, 32)

        @block.gpsimd
        def _(pool):
            pool.memset(x[:, T - 1, :], 0.0).then_inc(zero_set, 1)
            pool.memset(ones[:, :], 1.0).then_inc(set_pool, 1)
            pool.memset(packed, 0).then_inc(pad_set, 1)
            pool.memset(gloc_i, P * PACK + N).then_inc(pad_set, 1)
            BEFORE = (0, C_SCAT[0] // SB // 2)

            def scatter_half(l, i, h, size=SB, rounds_before=None, first=0):
                before = BEFORE[l] if rounds_before is None else rounds_before
                hold("pool", pool, scattered[h], (i * size + before * SB) * 16)
                at_ = bass.ds((i * 2 + h) * size + first, size)
                pool.tensor_copy(stg_place[:, h, 0:size], place[:, l, at_]).then_inc(staged, 1)
                pool.tensor_copy(stg_load[:, h, 0:size], load[:, l, at_]).then_inc(staged, 1)
                hold("pool", pool, staged, ((i + before) * 2 + h + 1) * 2)

                def scatter(b):
                    pool.indirect_dma_start(
                        sorted_edges[l][:, :], bass.IndirectOffsetOnAxis(ap=stg_place[:, h, b:b + 1], axis=0),
                        stg_load[:, h, b:b + 1], None, bounds_check=P * KS - 1, oob_is_err=False,
                    ).then_inc(scattered[h], 16)
                return scatter

            def scatter_edges(l, n):
                pool.wait_ge(edges_placed, l + 1)

                def body(i):
                    for h in range(2):
                        scatter = scatter_half(l, i, h)
                        for b in range(SB):
                            scatter(b)
                rounds(pool, n, body)

            def gather(l, table):

                def body(i):
                    for h in range(2):
                        hold("pool", pool, staged_g[l], i * 2 + (h + 1))
                        for b in range(GB):
                            pool.indirect_dma_start(
                                gath[l][h * GB + b][:, 0:D], None, table[:, :],
                                bass.IndirectOffsetOnAxis(ap=stg_g[:, h, b:b + 1], axis=0),
                            ).then_inc(gathered[l][h * GB + b], 16)
                rounds(pool, KS // GB // 2, body)

            def slots(l):
                g = l * KM
                pool.wait_ge(tokens_placed, l + 1)
                pool.wait_ge(hn_stored[2 * l], 16 * T // TG)

                def tokens_in(index, j):
                    pool.indirect_dma_start(xs[:, j, :], None, hn_tables[2 * l][:, :],
                                            bass.IndirectOffsetOnAxis(ap=index, axis=0)).then_inc(xs_in[j], 16)

                def body(i, last=False):
                    for j in range(XB):
                        k = i * XB + j
                        hold("pool", pool, xs_turned, k + (g + 1))
                        hold("pool", pool, ys_stored[j % 2], (i * 2 + (j // 2 - 1 + g // 2)) * 16)
                        pool.tensor_copy(stg_tok[:, j:j + 1, :], tok_rows[:, bass.ds(k + XB, 1), :]
                                         ).then_inc(tok_staged, 1)
                        hold("pool", pool, tok_staged, k + (g + 1))
                        if not last:
                            tokens_in(stg_tok[:, j, 0:1], j)
                        if l == 0:
                            if j % 2 == 0:
                                scatter = scatter_half(1, i, j // 2, 2 * ST, BEFORE[1] + SCAT_EARLY, SCAT_EARLY * 2 * SB)
                            for b in range(ST):
                                scatter(j % 2 * ST + b)
                        hold("pool", pool, y_out, k + (g + 1))
                        pool.indirect_dma_start(
                            results[:, :], bass.IndirectOffsetOnAxis(ap=stg_tok[:, j, 1:2], axis=0), ys[:, j % 2, :],
                            None, bounds_check=CM * P - 1, oob_is_err=False).then_inc(ys_stored[j % 2], 16)

                for k in range(XB):
                    tokens_in(tok_rows[:, k, 0:1], k)
                n = KM // XB
                rounds(pool, n - 1, body)
                body(n - 1, last=True)

            pool.wait_ge(lists_init, 32)
            scatter_edges(0, C_SCAT[0] // SB // 2)
            pool.wait_ge(list_ready, 1)
            pool.wait_ge(rel_stored[0], 16 * (T // 2 + 1))
            pool.wait_ge(rel_stored[1], 16 * (T // 2))
            gather(0, rel_table)
            scatter_edges(1, SCAT_EARLY)
            slots(0)
            pool.wait_ge(list_ready, 2)
            pool.wait_ge(hn_stored[1], 16 * T // TG)
            gather(1, hn_tables[1])
            pool.wait_ge(h_stored, 16 * T // TG)
            gather(2, h_table)
            slots(1)

        @block.scalar
        def _(act):
            def std(n):
                act.wait_ge(var_out, n)
                act.activation(rstd[:, :], rstd[:, :], ACT.Sqrt).then_inc(std_out, 1)

            def turn(n, used, per=1, base=0):
                def body(t, j):
                    hold("act", act, turned, t + (n * T + 1))
                    if not isinstance(t, int) or t >= 2:
                        hold("act", act, used, (t - 1) * per + base)
                    act.copy(hT[:, j, :, :].rearrange("p k d -> p (k d)"), ps[:, 6 + j, 0:D]).then_inc(turned_in, 1)
                return body

            def rel_part(t, j):
                turn(0, rel_mm, 4)(t, j)
                hold("act", act, rel_stored[j], (t - j) * 8)
                for g in range(4):
                    hold("act", act, rel_mm, t * 4 + g + 1)
                    act.copy(rel_out[:, j, g * 512:(g + 1) * 512], ps[:, g, :]).then_inc(rel_copied, 1)

            def softmax_exp(n):
                act.wait_ge(lgm_out, n)
                act.activation(lg[:, 1, :, :], lg[:, 1, :, :], ACT.Exp).then_inc(exp_out, 1)

            def experts(l):
                g = l * KM

                def xsT_copy(k, j):
                    hold("act", act, xs_turned, k + (g + 1))
                    hold("act", act, h_mm, k + (g - 1))
                    act.copy(xsT[:, j, :, :].rearrange("p k d -> p (k d)"), ps[:, 5, 0:D]).then_inc(xsT_in, 1)

                def slot(k, j, last=False):
                    hold("act", act, h_mm, k + (g + 1))
                    if l == 0:
                        hold("act", act, hid_turned, k)
                        act.activation(hid.rearrange("p (b h) -> p b h", b=2), ps[:, 0:2, 0:HH], ACT.Silu
                                       ).then_inc(act_out, 1)
                    else:
                        hold("act", act, hid_turned, k + g)
                        act.activation(hid[:, 0:D], ps[:, 0, 0:D], ACT.Gelu).then_inc(hid_out, 1)
                    if not last:
                        xsT_copy(k + 1, 1 - j)
                    hold("act", act, hid_turned, k + (g + 1))
                    hold("act", act, y_mm, k + (g - 1))
                    if l == 0:
                        act.copy(hidT[0:HC, j, 0:4, :], ps[0:HC, 6, :].rearrange("p (k d) -> p k d", k=4)
                                 ).then_inc(hidT_act, 1)
                    else:
                        act.copy(hidT[:, j, 0:2, :], ps[:, 6, 0:D].rearrange("p (k d) -> p k d", k=2)
                                 ).then_inc(hidT_act, 1)

                xsT_copy(0, 0)
                slot(0, 0)
                slot(1, 1)
                with act.Fori(1, KM // 2 - 1) as i:
                    slot(i * 2, 0)
                    slot(i * 2 + 1, 1)
                slot(KM - 2, 0)
                slot(KM - 1, 1, last=True)

            def root_part(tiles):
                for t in tiles:
                    turn(2, root_mm)(t, t % 2)
                    if t > tiles[0]:
                        root_copy(t - 1)
                root_copy(tiles[-1])

            def root_copy(t):
                act.wait_ge(root_mm, t + 1)
                act.copy(root[:, t, :], ps[:, t % 2, 0:D]).then_inc(root_out, 1)

            def neigh_part(t, j):
                turn(3, neigh_mm)(t, j)
                if not isinstance(t, int) or t:
                    relu(t - 1)

            def relu(t):
                hold("act", act, pre_out, t + 1)
                act.activation(root[:, bass.ds(t, 1), :], root[:, bass.ds(t, 1), :], ACT.Relu).then_inc(h_out, 1)

            def stage(l, first=0, end=KS // GB // 2):

                def squares(i, h):
                    for b in range(h * GB, (h + 1) * GB):
                        hold("act", act, gathered[l][b], (i + 1) * 16)
                        act.activation(gath[l][b][:, D:2 * D], gath[l][b][:, 0:D], ACT.Square).then_inc(squared, 1)

                def body(i):
                    for h in range(2):
                        if not isinstance(i, int):
                            hold("act", act, summed[l], i * (2 * GB) + (h - 1) * GB)
                        act.copy(stg_g[:, h, 0:GB], gidx[:, bass.ds((i * 2 + h) * GB, GB)]).then_inc(staged_g[l], 1)
                        if l == 2 and h == 1:
                            squares(i, 0)
                        elif l == 2 and not isinstance(i, int):
                            squares(i - 1, 1)
                if first == 0:
                    act.wait_ge(list_ready, 1 if l == 0 else 2)
                if end == 1:
                    body(0)
                else:
                    rounds(act, end, body, first)
                if l == 2:
                    squares(end - 1, 1)

            std(1)
            pairs(act, rel_part)
            stage(0)
            std(2)
            pairs(act, turn(1, routed))
            softmax_exp(1)
            experts(0)
            std(3)
            stage(1, end=1)
            for part in range(len(PARTS) - 1):
                root_part(range(part * TG, (part + 1) * TG))
                stage(1, PARTS[part] + 1, min(PARTS[part + 1] + 1, PARTS[-1]))
            pairs(act, neigh_part)
            relu(T - 1)
            stage(2)
            for t in range(T):
                act.wait_ge(gg_out, t // TG + 1)
                act.activation(accx[:, t, 0:D], accx[:, t, 0:D], ACT.Tanh, scale=deg[:, 1, t:t + 1]).then_inc(tanh_out, 1)
            std(4)
            pairs(act, turn(4, routed, base=T))
            softmax_exp(2)
            experts(1)

        @block.tensor
        def _(pe):
            pe.wait_ge(consts_in, 64)
            pe.wait_ge(set_pool, 1)

            def count(n, buckets):
                pe.wait_ge(ranked, n)
                pe.matmul(ps[:, 4, 416:416 + buckets], below, cnt[:, 0, 0:buckets], start=True, stop=True)
                pe.matmul(ps[:, 4, 464:464 + buckets], ones[:, :], cnt[:, 0, 0:buckets], start=True, stop=True
                          ).then_inc(counted, 1)

            def turned_tiles(n, source, use, first=0, end=T):
                def turn(t):
                    if t >= 2:
                        pe.wait_ge(turned_in, n * T + t - 1)
                    for k in range(2):
                        last = pe.transpose(ps[:, 6 + t % 2, k * P:(k + 1) * P], source(t, k), ident)
                    last.then_inc(turned, 1)
                turn(first)
                for t in range(first, end):
                    if t + 1 < end:
                        turn(t + 1)
                    pe.wait_ge(turned_in, n * T + t + 1)
                    use(t, t % 2)

            def hn_half(t, k):
                return hn[:, t, k * P:(k + 1) * P]

            def rel_tile(t, j):
                for g in range(4):
                    if t:
                        pe.wait_ge(rel_copied, 4 * (t - 1) + g + 1)
                    for k in range(2):
                        last = pe.matmul(ps[:, g, :], hT[:, j, k, :],
                                         w_rel[:, k, 2 * g:2 * g + 2, :].rearrange("p a b -> p (a b)"),
                                         start=(k == 0), stop=(k == 1))
                    last.then_inc(rel_mm, 1)
                    if t >= PERM_FROM:
                        n, groups = CP // PB // 2, (T - PERM_FROM) * 4
                        q = (t - PERM_FROM) * 4 + g
                        permute(q * n // groups, (q + 1) * n // groups)
                if t in (COUNT_1, COUNT_2):
                    count(1 if t == COUNT_1 else 2, T)

            def permute(first, end):
                n = CP // PB // 2

                def body(i):
                    for h in range(2):
                        hold("pe", pe, perm_out, i * 2 + (h + 1))
                        for b in range(h * PB, (h + 1) * PB):
                            for part in range(2):
                                last = pe.matmul(ps[:, 4 + part, 0:KS], perm_row[:, b, part, :], perm_col[:, b, :],
                                                 start=(isinstance(i, int) and i == 0 and b == 0),
                                                 stop=(isinstance(i, int) and i == n - 1 and b == 2 * PB - 1))
                            last.then_inc(permuted, 1)
                for i in range(first, end):
                    body(i)

            def router_tile(l):
                def use(t, j):
                    for k in range(2):
                        last = pe.matmul(ps[:, 4, t * X:(t + 1) * X], hT[:, j, k, :], rw[:, l, k, :],
                                         start=(k == 0), stop=(k == 1))
                    last.then_inc(routed, 1)
                return use

            def root_tile(t, j):
                if t >= 2:
                    pe.wait_ge(root_out, t - 1)
                for k in range(2):
                    pe.matmul(ps[:, j, 0:D], hT[:, j, k, :], w_root[:, k, :], start=(k == 0), stop=False)
                pe.matmul(ps[:, j, 0:D], ones[0:1, :], bias1, start=False, stop=True).then_inc(root_mm, 1)

            def neigh_tile(t, j):
                if t >= 2:
                    pe.wait_ge(pre_out, t - 1)
                for k in range(2):
                    last = pe.matmul(ps[:, 2 + j, 0:D], hT[:, j, k, :], w_neigh[:, k, :], start=(k == 0), stop=(k == 1))
                last.then_inc(neigh_mm, 1)

            def edge_sums(l, first=0, end=KS // GB // 2):
                w = width[l]

                def body(i):
                    for h in range(2):
                        hold("pe", pe, hot_out[l], i * 2 + (h + 1))
                        for b in range(h * GB, (h + 1) * GB):
                            hold("pe", pe, gathered[l][b], (i + 1) * 16)
                            if l == 2:
                                hold("pe", pe, squared, i * (2 * GB) + (b + 1))
                            k = i * (2 * GB) + b
                            if not isinstance(i, int) or k >= 8:
                                hold("pe", pe, added[l], k - 7)
                            pe.matmul(ps[:, b % 8, 0:w], hot[l][:, b, :], gath[l][b][:, 0:w],
                                      start=True, stop=True).then_inc(summed[l], 1)
                rounds(pe, end, body, first)

            def place_tokens(l):
                pe.wait_ge(hots_out, l + 1)
                for c in range(CM):
                    last = pe.matmul(ps[:, 5, 0:KM], hot_rows[l][:, c, :], hot_cols[l][:, c, :],
                                     start=(c == 0), stop=(c == CM - 1))
                last.then_inc(tok_permuted, 1)

            def experts(l):
                g = l * KM

                def xs_turn(k, j):
                    hold("pe", pe, xs_in[j], (k - j + XB + g) * (16 // XB))
                    hold("pe", pe, xsT_in, k + g)
                    for c in range(2):
                        last = pe.transpose(ps[:, 5, c * P:(c + 1) * P], xs[:, j, c * P:(c + 1) * P], ident)
                    last.then_inc(xs_turned, 1)

                def hidden(k, j, e):
                    hold("pe", pe, xsT_in, k + (g + 1))
                    hold("pe", pe, hid_out, k + g)
                    if l == 0:
                        for w in range(2):
                            for b in range(2):
                                for c in range(2):
                                    last = pe.matmul(ps[:, 2 * w + b, 0:HH], xsT[:, j, c, :],
                                                     w13[:, 2 * w + c, bass.ds(e * H0 + b * HH, HH)],
                                                     start=(c == 0), stop=(c == 1))
                    else:
                        for c in range(2):
                            pe.matmul(ps[:, 0, 0:D], xsT[:, j, c, :], e1w1[:, c, bass.ds(e * D, D)],
                                      start=(c == 0), stop=False)
                        last = pe.matmul(ps[:, 0, 0:D], ones[0:1, :], e1b[:, 0, bass.ds(e * D, D)],
                                         start=False, stop=True)
                    last.then_inc(h_mm, 1)

                def results(k, j, e):
                    hold("pe", pe, hidT_act, k + (g + 1))
                    if l == 0:
                        hold("pe", pe, hidT_dve, k + 1)
                    hold("pe", pe, y_out, k + g)
                    if l == 0:
                        for c in range(NHC):
                            n = min(HC, H0 - c * HC)
                            last = pe.matmul(ps[:, 4, 0:D], hidT[0:n, j, c, :], w2[c][0:n, bass.ds(e * D, D)],
                                             start=(c == 0), stop=(c == NHC - 1))
                    else:
                        for c in range(2):
                            pe.matmul(ps[:, 4, 0:D], hidT[:, j, c, :], e1w2[:, c, bass.ds(e * D, D)],
                                      start=(c == 0), stop=False)
                        last = pe.matmul(ps[:, 4, 0:D], ones[0:1, :], e1b[:, 1, bass.ds(e * D, D)],
                                         start=False, stop=True)
                    last.then_inc(y_mm, 1)

                def hidden_turn(k):
                    hold("pe", pe, hid_out, k + (g + 1))
                    for c in range(NHC if l == 0 else 2):
                        n = min(HC, H0 - c * HC) if l == 0 else P
                        step = HC if l == 0 else P
                        last = pe.transpose(ps[0:n, 6 + c // 4, (c % 4) * P:(c % 4 + 1) * P],
                                            hid[:, c * step:c * step + n], ident)
                    last.then_inc(hid_turned, 1)

                def expert(k):
                    return pe.value_load(expert_of[0:1, bass.ds(k, 1)], min_val=0, max_val=X - 1)

                def slot(k, j, last=False):
                    hidden(k, j % 2, expert(k))
                    if not isinstance(k, int) or k:
                        results(k - 1, (j + 1) % 2, expert(k - 1))
                    if not last:
                        xs_turn(k + 1, (j + 1) % XB)
                    hidden_turn(k)

                pe.wait_ge(tokens_placed, l + 1)
                if l == 0:
                    pe.wait_ge(w13_in, 64 * X)
                    pe.wait_ge(w2_in, 16 * NHC)
                else:
                    pe.wait_ge(e1_in, 96)
                xs_turn(0, 0)
                for j in range(XB):
                    slot(j, j)
                with pe.Fori(1, KM // XB - 1) as i:
                    for j in range(XB):
                        slot(i * XB + j, j)
                for j in range(XB):
                    slot(KM - XB + j, j, last=(j == XB - 1))
                results(KM - 1, 1, expert(KM - 1))

            pe.wait_ge(w_rel_out, 1)
            pe.wait_ge(normed, T)
            turned_tiles(0, hn_half, rel_tile)
            pe.wait_ge(list_ready, 1)
            edge_sums(0)
            pe.wait_ge(rw_in, 16)
            pe.wait_ge(normed, 2 * T)
            turned_tiles(1, hn_half, router_tile(0))
            count(3, X)
            place_tokens(0)
            experts(0)
            pe.wait_ge(normed, 3 * T)
            pe.wait_ge(wl_in, 48)
            for part in range(len(PARTS) - 1):
                if part:
                    pe.wait_ge(added[1], PARTS[part] * 2 * GB)
                turned_tiles(2, hn_half, root_tile, part * TG, (part + 1) * TG)
                pe.wait_ge(root_out, (part + 1) * TG)
                edge_sums(1, PARTS[part], PARTS[part + 1])
            pe.wait_ge(added[1], KS)
            turned_tiles(3, lambda t, k: accx[:, t, k * P:(k + 1) * P], neigh_tile)
            edge_sums(2)
            pe.wait_ge(normed, 4 * T)
            turned_tiles(4, hn_half, router_tile(1))
            count(4, X)
            place_tokens(1)
            experts(1)

        @block.vector
        def _(dve):
            steps = [0]

            def then(ins):
                steps[0] += 1
                ins.then_inc(dve_step, 1)
                dve.wait_ge(dve_step, steps[0])

            def also(ins):
                steps[0] += 1
                ins.then_inc(dve_step, 1)

            def over_p(row, n):
                return row.unsqueeze(2).to_broadcast([row.shape[0], row.shape[1], n])

            def over_n(row, n):
                return row.unsqueeze(1).to_broadcast([row.shape[0], n, row.shape[1]])

            def rank_items(buckets, b, c, hots, scans, hots_flat, scans_flat, result):
                for j in range(b):
                    also(dve.tensor_scalar(hots[:, j, :], buckets, float(j), None, ALU.is_equal))
                dve.wait_ge(dve_step, steps[0])
                then(dve.tensor_tensor_scan(scans_flat, hots_flat, hots_flat, 0.0, ALU.add, ALU.max))
                then(dve.tensor_copy(upto[:, 1:b + 1], scans[:, :, c - 1]))
                dve.tensor_tensor(cnt[:, 0, 0:b], upto[:, 1:b + 1], upto[:, 0:b], ALU.subtract).then_inc(ranked, 1)
                count_no[0] += 1
                dve.wait_ge(counted, count_no[0])
                then(dve.tensor_scalar(cnt_i[:, 0:b], ps[:, 4, 464:464 + b], float(P - 1), None, ALU.add))
                then(dve.tensor_scalar(cnt_i[:, 0:b], cnt_i[:, 0:b], 65535 - (P - 1), None, ALU.bitwise_and))
                then(dve.tensor_copy(cnt[:, 1, 0:b], cnt_i[:, 0:b]))
                then(dve.tensor_tensor_scan(cnt[:, 2, 0:b], cnt[:, 1, 0:b], cnt[:, 1, 0:b], 0.0, ALU.add, ALU.max))
                then(dve.tensor_tensor(cnt[:, 3, 0:b], cnt[:, 2, 0:b], cnt[:, 1, 0:b], ALU.subtract))
                then(dve.tensor_tensor(cnt[:, 3, 0:b], cnt[:, 3, 0:b], ps[:, 4, 416:416 + b], ALU.add))
                then(dve.scalar_tensor_tensor(cnt[:, 3, 0:b], cnt[:, 3, 0:b], -1.0, upto[:, 0:b], ALU.add, ALU.subtract))
                for j in range(b):
                    also(dve.scalar_tensor_tensor(scans[:, j, :], scans[:, j, :], cnt[:, 3, j:j + 1], hots[:, j, :],
                                                  ALU.add, ALU.mult))
                dve.wait_ge(dve_step, steps[0])
                then(dve.tensor_reduce(result, scans.rearrange("p b c -> p c b"), AX_X, ALU.add))

            count_no = [0]

            def slot_experts(b, n, compare, result):
                ends = cnt[0:1, 2, 0:b]
                cmp = compare.rearrange("p (k b) -> p k b", b=b)
                then(dve.tensor_tensor(cmp, over_n(ends, n), over_p(tok_starts, b), ALU.is_le))
                then(dve.tensor_reduce(scan_row[:, 0:n], cmp, AX_X, ALU.add))
                then(dve.tensor_scalar(result, scan_row[:, 0:n], float(b - 1), None, ALU.min))

            scan_row = gloc[0:1, :]

            def slot_blocks(l):
                cmp = scan_sort[:, 0:BPW, 0:T]
                then(dve.tensor_tensor(cmp, over_n(cnt[:, 2, 0:T], BPW), over_p(word_starts, T), ALU.is_le))
                of = slot_word[:, l, :]
                then(dve.tensor_reduce(of, cmp, AX_X, ALU.add))
                then(dve.tensor_scalar(of, of, float(T - 1), None, ALU.min))
                for j in range(BPW - 2, -1, -1):
                    then(dve.scalar_tensor_tensor(of[:, j:j + 1], of[:, j + 1:j + 2], float(T), of[:, j:j + 1],
                                                  ALU.mult, ALU.add))
                dve.tensor_copy(slot_word_i[:, l:l + 1], of[:, 0:1]).then_inc(word_out, 1)

            def read_edges():
                dve.wait_ge(edges_in, 48)
                src, dst, et = (raw[:, i, :] for i in range(3))
                for l, to in ((0, dst), (1, src)):
                    then(dve.tensor_scalar(work_i[:, 0, :], to, 7, None, ALU.logical_shift_right))
                    dve.tensor_copy(bucket[:, l, :], work_i[:, 0, :])
                    then(dve.tensor_scalar(work_i[:, 1 + l, :], to, P - 1, None, ALU.bitwise_and))
                then(dve.scalar_tensor_tensor(work_f[:, 0, :], src, float(NREL), et, ALU.mult, ALU.add))
                then(dve.tensor_scalar(work_f[:, 0, :], work_f[:, 0, :], -1.0, float(N * NREL), ALU.mult, ALU.add))
                then(dve.tensor_scalar(work_f[:, 0, :], work_f[:, 0, :], 0.0, None, ALU.max))
                then(dve.scalar_tensor_tensor(load[:, 0, :], work_i[:, 1, :], float(PACK), work_f[:, 0, :],
                                              ALU.mult, ALU.add))
                then(dve.scalar_tensor_tensor(load[:, 1, :], work_i[:, 2, :], float(PACK), dst, ALU.mult, ALU.add))

            def sort_edges(l):
                rank_items(bucket[:, l, :], T, C, hot_sort, scan_sort, hot_flat, scan_flat, sort_f[:, 0, :])
                then(dve.tensor_copy(sort_i[:, 0, :], sort_f[:, 0, :]))
                then(dve.tensor_scalar(sort_i[:, 1, :], sort_i[:, 0, :], P - 1, None, ALU.bitwise_and))
                then(dve.tensor_scalar(sort_i[:, 0, :], sort_i[:, 0, :], 7, None, ALU.logical_shift_right))
                then(dve.tensor_scalar(sort_f[:, 1, :], bucket[:, l, :], float(T), SKIP, ALU.is_ge, ALU.mult))
                if l == 0:
                    rest = slice(C_SCAT[0], C)
                    then(dve.tensor_copy(row_of, sort_i[:, 1, rest]))
                    then(dve.tensor_tensor(col_of, sort_i[:, 0, rest], sort_f[:, 1, rest], ALU.add))
                    then(dve.tensor_scalar(part_i, load[:, 0, rest], HALF_BITS, None, ALU.logical_shift_right))
                    then(dve.tensor_copy(part_a, part_i))
                    then(dve.tensor_scalar(part_i, load[:, 0, rest], (1 << HALF_BITS) - 1, None, ALU.bitwise_and))
                    then(dve.tensor_copy(part_b, part_i))
                then(dve.scalar_tensor_tensor(sort_f[:, 0, :], sort_i[:, 1, :], float(KS), sort_i[:, 0, :],
                                              ALU.mult, ALU.add))
                then(dve.tensor_tensor(place[:, l, :], sort_f[:, 0, :], sort_f[:, 1, :], ALU.add))
                dve.sem_inc(edges_placed, 1)
                slot_blocks(l)

            def permute():
                def body(i):
                    for h in range(2):
                        if not isinstance(i, int):
                            hold("dve", dve, permuted, i * (2 * PB) + (h - 1) * PB)
                        for b in range(h * PB, (h + 1) * PB):
                            c = bass.ds(i * (2 * PB) + b, 1)
                            dve.tensor_scalar(perm_col[:, b, :], count_cols, col_of[:, c], None, ALU.is_equal)
                            for part, of in enumerate((part_a, part_b)):
                                last = dve.tensor_scalar(perm_row[:, b, part, :], count_rows, row_of[:, c], of[:, c],
                                                         ALU.is_equal, ALU.mult)
                        last.then_inc(perm_out, 1)
                rounds(dve, CP // PB // 2, body)

            sort_f = at(0, 2, C)
            sort_i = at(2 * C, 2, C, dt=I32)

            def relation_weights():
                dve.wait_ge(wc_in, 16 * NREL)
                for k in range(2):
                    dve.wait_ge(basis_in[k], 16 * NREL)
                    then(dve.tensor_scalar(w_rel[:, k, :, :], basis_sb[k][:, :, 0, :], wc[:, 0:1], None, ALU.mult))
                    for b in range(1, NBASES):
                        then(dve.scalar_tensor_tensor(w_rel[:, k, :, :], basis_sb[k][:, :, b, :], wc[:, b:b + 1],
                                                      w_rel[:, k, :, :], ALU.mult, ALU.add))
                dve.sem_inc(w_rel_out, 1)

            def layer_norm(n):
                U = 5
                with dve.Fori(0, T // U) as i:
                    for u in range(U):
                        t = i * U + u
                        dve.bn_stats(stats[:, bass.ds(t, 1), :].rearrange("p a b -> p (a b)"),
                                     x[:, bass.ds(t, 1), :].rearrange("p a b -> p (a b)")).then_inc(stat_out, 1)
                dve.wait_ge(stat_out, n * T)
                then(dve.tensor_tensor(mean[:, :], stats[:, :, 1], stats[:, :, 4], ALU.add))
                then(dve.tensor_tensor(rstd[:, :], stats[:, :, 1], stats[:, :, 4], ALU.subtract))
                then(dve.tensor_tensor(rstd[:, :], rstd[:, :], rstd[:, :], ALU.mult))
                then(dve.tensor_scalar(rstd[:, :], rstd[:, :], 0.25, EPS, ALU.mult, ALU.add))
                then(dve.tensor_tensor(stats[:, :, 2], stats[:, :, 2], stats[:, :, 5], ALU.add))
                then(dve.scalar_tensor_tensor(rstd[:, :], stats[:, :, 2], 1.0 / D, rstd[:, :], ALU.mult, ALU.add))
                dve.tensor_scalar(mean[:, :], mean[:, :], 0.5, None, ALU.mult).then_inc(var_out, 1)
                dve.wait_ge(std_out, n)
                then(dve.reciprocal(rstd[:, :], rstd[:, :]))
                with dve.Fori(0, T // U) as i:
                    for u in range(U):
                        t = bass.ds(i * U + u, 1)
                        dve.tensor_scalar(hn[:, t, :], x[:, t, :], mean[:, t], rstd[:, t],
                                          ALU.subtract, ALU.mult).then_inc(normed, 1)

            def unpack(l):
                dve.wait_ge(list_in, 16 * (l + 1))
                if l == 0:
                    dve.wait_ge(permuted, CP)
                    then(dve.tensor_copy(gloc[:, :], packed))
                    then(dve.tensor_tensor(gloc[:, :], gloc[:, :], ps[:, 5, 0:KS], ALU.add))
                    then(dve.scalar_tensor_tensor(packed, ps[:, 4, 0:KS], float(1 << HALF_BITS), gloc[:, :],
                                                  ALU.mult, ALU.add))
                then(dve.tensor_scalar(gidx[:, :], packed, PACK - 1, None, ALU.bitwise_and))
                if l == 0:
                    then(dve.tensor_scalar(gidx[:, :], gidx[:, :], -1.0, float(N * NREL), ALU.mult, ALU.add))
                then(dve.tensor_scalar(gloc_i, packed, 15, None, ALU.logical_shift_right))
                then(dve.tensor_copy(gloc[:, :], gloc_i))
                dve.sem_inc(list_ready, 1)

            def edge_sums(l):
                w, lst = width[l], min(l, 1)

                def one_hot(i, h):
                    if not isinstance(i, int):
                        hold("dve", dve, summed[l], i * (2 * GB) + (h - 1) * GB)
                    nodes = gloc[:, bass.ds((i * 2 + h) * GB, GB)]
                    dve.tensor_tensor(hot[l][:, h * GB:(h + 1) * GB, :], over_n(lane, GB), over_p(nodes, P),
                                      ALU.is_equal).then_inc(hot_out[l], 1)

                def add(i, h):
                    for b in range(h * GB, (h + 1) * GB):
                        k = i * (2 * GB) + b
                        if b % BPW == 0:
                            word = i * (2 * GB // BPW) + b // BPW
                            blocks = dve.value_load(block_of[0:1, lst, bass.ds(word, 1)], min_val=0, max_val=T ** BPW - 1)
                            hold("dve", dve, summed[l], k + BPW)
                        blk = (blocks // T ** (b % BPW)) % T
                        hold("dve", dve, added[l], k)
                        to = acc[l][:, bass.ds(blk, 1), 0:w]
                        dve.tensor_tensor(to, to, ps[:, b % 8:b % 8 + 1, 0:w], ALU.add).then_inc(added[l], 1)

                def body(i):
                    one_hot(i, 0)
                    if not isinstance(i, int):
                        add(i - 1, 1)
                    one_hot(i, 1)
                    add(i, 0)
                n = KS // GB // 2
                rounds(dve, n, body)
                add(n - 1, 1)
                dve.wait_ge(added[l], KS)

            def route(l):
                flat = [lg[:, i, :, :] for i in range(4)]
                dve.wait_ge(routed, (l + 1) * T)
                then(dve.tensor_copy(flat[0].rearrange("p a b -> p (a b)"), ps[:, 4, 0:T * X]))
                then(dve.tensor_reduce(tops[:, 0, :], flat[0], AX_X, ALU.max))
                dve.tensor_tensor(flat[1], flat[0], over_p(tops[:, 0, :], X), ALU.subtract).then_inc(lgm_out, 1)
                dve.wait_ge(exp_out, l + 1)
                then(dve.tensor_reduce(tops[:, 0, :], flat[1], AX_X, ALU.add))
                then(dve.reciprocal(tops[:, 0, :], tops[:, 0, :]))
                then(dve.tensor_tensor(flat[1], flat[1], over_p(tops[:, 0, :], X), ALU.mult))
                for c in range(TOPK):
                    then(dve.tensor_reduce(gates[:, c, :], flat[1], AX_X, ALU.max))
                    then(dve.tensor_tensor(flat[2], flat[1], over_p(gates[:, c, :], X), ALU.is_equal))
                    then(dve.scalar_tensor_tensor(flat[2], flat[2], -float(X), over_n(iota_x8, T), ALU.mult, ALU.add))
                    then(dve.tensor_reduce(choice[:, c, :], flat[2], AX_X, ALU.min))
                    if c + 1 < TOPK:
                        then(dve.tensor_tensor(flat[2], over_n(iota_x, T), over_p(choice[:, c, :], X), ALU.is_equal))
                        then(dve.scalar_tensor_tensor(flat[1], flat[2], -2.0, flat[1], ALU.mult, ALU.add))
                then(dve.tensor_tensor(tops[:, 1, :], gates[:, 0, :], gates[:, 1, :], ALU.add))
                if l == 0:
                    then(dve.tensor_scalar(tops[:, 1, :], tops[:, 1, :], 1e-9, None, ALU.add))
                else:
                    then(dve.tensor_scalar(tops[:, 1, :], tops[:, 1, :], 1e-12, None, ALU.max))
                then(dve.reciprocal(tops[:, 1, :], tops[:, 1, :]))
                then(dve.tensor_tensor(gates[:, :, :], gates[:, :, :], over_n(tops[:, 1, :], TOPK), ALU.mult))
                then(dve.tensor_tensor(choice[:, :, :], choice[:, :, :], over_n(beyond, TOPK), ALU.add))
                ch = choice[:, :, :].rearrange("p a b -> p (a b)")
                m0, m1 = (msort[:, i, :, :] for i in range(2))
                rank_items(ch, X, CM, m0, m1, m0.rearrange("p a b -> p (a b)"), m1.rearrange("p a b -> p (a b)"),
                           rank[:, :])
                then(dve.tensor_scalar(ch, ch, float(X), SKIP, ALU.is_ge, ALU.mult))
                then(dve.tensor_copy(place_i[:, 0, :], rank[:, :]))
                then(dve.tensor_scalar(place_i[:, 1, :], place_i[:, 0, :], 7, None, ALU.logical_shift_right))
                then(dve.tensor_scalar(place_i[:, 0, :], place_i[:, 0, :], P - 1, None, ALU.bitwise_and))
                then(dve.tensor_copy(place_f[:, :, :], place_i[:, :, :]))
                then(dve.tensor_tensor(place_f[:, 1, :], place_f[:, 1, :], ch, ALU.add))
                also(dve.tensor_tensor(hot_rows[l], over_n(lane, CM), over_p(place_f[:, 0, :], P), ALU.is_equal))
                then(dve.tensor_tensor(hot_cols[l], over_n(slot_no, CM), over_p(place_f[:, 1, :], KM), ALU.is_equal))
                dve.tensor_tensor(hot_cols[l], hot_cols[l], over_p(choice_id, KM), ALU.mult).then_inc(hots_out, 1)
                cm2 = msort[0:1, :, :, :].rearrange("p j a b -> p (j a b)")[:, 0:KM * X]
                slot_experts(X, KM, cm2, expert_of[:, :])
                dve.wait_ge(tok_permuted, l + 1)
                ids, empty, back_to = (slot_tok[:, i, :] for i in range(3))
                then(dve.tensor_copy(ids, ps[:, 5, 0:KM]))
                then(dve.tensor_scalar(empty, ids, 0.0, SKIP, ALU.is_equal, ALU.mult))
                also(dve.scalar_tensor_tensor(tok_rows[:, XB:, 1], ids, -1.0, empty, ALU.add, ALU.add))
                then(dve.tensor_scalar(back_to, ids, NP + 1.0, float(NP), ALU.is_ge, ALU.mult))
                then(dve.scalar_tensor_tensor(back_to, ids, -1.0, back_to, ALU.add, ALU.subtract))
                then(dve.tensor_scalar(tok_rows[:, 0:KM, 0], back_to, 0.0, None, ALU.max))
                dve.sem_inc(tokens_placed, 1)

            def experts(l):
                g = l * KM

                def slot(k, j, first=False):
                    if l == 0:
                        hold("dve", dve, act_out, k + 1)
                        dve.tensor_tensor(hid.rearrange("p (b h) -> p b h", b=2), hid.rearrange("p (b h) -> p b h", b=2),
                                          ps[:, 2:4, 0:HH], ALU.mult).then_inc(hid_out, 1)
                    if not first:
                        result(k - 1, 1 - j)
                    if l == 0:
                        hold("dve", dve, hid_turned, k + 1)
                        hold("dve", dve, y_mm, k - 1)
                        dve.tensor_copy(hidT[0:HC, j, 4:NHC, :],
                                        ps[0:HC, 7, 0:(NHC - 4) * P].rearrange("p (k d) -> p k d", k=NHC - 4)
                                        ).then_inc(hidT_dve, 1)

                def result(k, j):
                    hold("dve", dve, y_mm, k + (g + 1))
                    hold("dve", dve, ys_stored[j], (k - j + g) * 8)
                    dve.tensor_copy(ys[:, j, :], ps[:, 4, 0:D]).then_inc(y_out, 1)
                slot(0, 0, first=True)
                slot(1, 1)
                with dve.Fori(1, KM // 2) as i:
                    slot(i * 2, 0)
                    slot(i * 2 + 1, 1)
                result(KM - 1, 1)

            def add_tanh(t):
                dve.wait_ge(tanh_out, t + TG)
                dve.tensor_tensor(x[:, t:t + TG, :], x[:, t:t + TG, :], accx[:, t:t + TG, 0:D], ALU.add
                                  ).then_inc(tanh_added, 1)

            def combine(l):
                for c in range(CM):
                    if c % TG == 0:
                        parts = 2 if (c + TG) % T == 0 else 1
                        dve.wait_ge(back[c // TG], 16 * parts * (l + 1))
                    if c >= T:
                        dve.wait_ge(combined, l * CM + c - T + 1)
                    t, n = c % T, P if (c + 1) % T else N - (T - 1) * P
                    dve.scalar_tensor_tensor(x[0:n, t, :], y_back[0:n, c, :], gates[0:n, c // T, t:t + 1], x[0:n, t, :],
                                             ALU.mult, ALU.add).then_inc(combined, 1)
                dve.wait_ge(combined, (l + 1) * CM)
                dve.sem_inc(combined_all, 1)

            dve.wait_ge(consts_in, 64)
            then(dve.memset(upto[:, :], 0.0))
            then(dve.memset(tok_rows[:, :, :], 0))
            read_edges()
            dve.wait_ge(x_in, 32)
            layer_norm(1)
            relation_weights()
            sort_edges(0)
            sort_edges(1)
            permute()
            dve.wait_ge(words_in, 32)
            dve.wait_ge(turned_in, T)
            dve.wait_ge(bias_in, 16)
            then(dve.tensor_copy(acc0[:, :, :], over_n(bias0[:, :], T)))
            unpack(0)
            edge_sums(0)
            then(dve.scalar_tensor_tensor(x[:, :, :], acc0[:, :, :], 0.0, x[:, :, :], ALU.max, ALU.add))
            layer_norm(2)
            route(0)
            experts(0)
            combine(0)
            layer_norm(3)
            then(dve.memset(accx, 0.0))
            then(dve.memset(g1[:, :, D:D + 1], 1.0))
            unpack(1)
            edge_sums(1)
            then(dve.tensor_copy(deg[:, 0, :], accx[:, :, D]))
            then(dve.tensor_scalar(deg[:, 1, :], deg[:, 0, :], 1.0, None, ALU.max))
            then(dve.reciprocal(deg[:, 1, :], deg[:, 1, :]))
            dve.wait_ge(root_out, T)

            def begin_sums(t):
                dve.wait_ge(h_out, t + 1)
                dve.scalar_tensor_tensor(acch[:, t, D:2 * D], root[:, t, :], deg[:, 0, t:t + 1], root[:, t, :],
                                         ALU.mult, ALU.mult).then_inc(begun, 1)

            dve.memset(acch[:, :, 0:D], 0.0).then_inc(begun, 1)
            for t in range(T):
                dve.wait_ge(neigh_mm, t + 1)
                dve.scalar_tensor_tensor(root[:, t, :], ps[:, 2 + t % 2, 0:D], deg[:, 1, t:t + 1], root[:, t, :],
                                         ALU.mult, ALU.add).then_inc(pre_out, 1)
                if t >= 2:
                    begin_sums(t - 2)
            begin_sums(T - 2)
            begin_sums(T - 1)
            dve.wait_ge(begun, T + 1)
            edge_sums(2)
            dve.wait_ge(h_stored, 16 * T // TG)
            for t in range(0, T, TG):
                tiles = slice(t, t + TG)
                g = accx[:, tiles, 0:D]
                then(dve.scalar_tensor_tensor(g, acch[:, tiles, 0:D], -2.0, root[:, tiles, :], ALU.mult, ALU.mult))
                dve.tensor_tensor(g, g, acch[:, tiles, D:2 * D], ALU.add).then_inc(gg_out, 1)
                if t:
                    add_tanh(t - TG)
            add_tanh(T - TG)
            dve.wait_ge(tanh_added, T // TG)
            dve.sem_inc(graph_done, 1)
            layer_norm(4)
            dve.wait_ge(normed, 4 * T)
            then(dve.tensor_tensor(x[:, :, :], x[:, :, :], hn[:, :, :], ALU.add))
            route(1)
            experts(1)
            combine(1)


def kernel(**inputs):
    import numpy as np
    import concourse.bacc as bacc
    from concourse.bass_utils import run_bass_kernel_spmd as run

    def c(name):
        return np.ascontiguousarray(inputs[name])

    def edges(name, fill):
        v = np.full(P * C, fill, np.int32)
        v[:E] = inputs[name]
        return v.reshape(P, C)

    i = np.arange(P)
    tiles = np.arange(T)
    small = np.concatenate([
        np.broadcast_to(tiles, (P, T)), np.broadcast_to(np.arange(X), (P, X)), np.broadcast_to(np.arange(X) + X, (P, X)),
        np.where(tiles[None, :] * P + i[:, None] >= N, 100, 0),
        np.arange(CM)[None, :] * P + i[:, None] + 1], 1).astype(np.float32)
    rw = np.stack([c("L0_ffn_router_w"), c("L1_ffn_router_w")])
    arrays = {
        "x": c("x"), "src": edges("src", NP), "dst": edges("dst", NP), "et": edges("edge_type_8", 0),
        "c_mats": np.concatenate([np.eye(P), i[:, None] < i[None, :], np.broadcast_to(i, (P, P))], 1).astype(np.float32),
        "c_small": small,
        "c_starts": np.concatenate([np.broadcast_to(np.arange(KM), (P, KM)),
                                    i[:, None] * BPW + np.arange(BPW), np.broadcast_to(np.arange(KM) / P, (P, KM))],
                                   1).astype(np.float32) * P,
        "c_count": np.broadcast_to(np.concatenate([np.arange(KS), i]), (P, KS + P)).astype(np.float16),
        "basis": c("L0_gnn_basis").reshape(NBASES * D, D), "w_comp": c("L0_gnn_w_comp"),
        "bias0": c("L0_gnn_bias").reshape(1, D), "bias1": c("L1_gnn_b").reshape(1, D),
        "rw": np.ascontiguousarray(rw.reshape(2, X, 2, P).transpose(3, 0, 2, 1)),
        "w1": np.ascontiguousarray(c("L0_ffn_w1").transpose(0, 2, 1)),
        "w3": np.ascontiguousarray(c("L0_ffn_w3").transpose(0, 2, 1)),
        "w2": np.ascontiguousarray(c("L0_ffn_w2").transpose(0, 2, 1)),
        "W_root": c("L1_gnn_W_root"), "W_neigh": c("L1_gnn_W_neigh"),
        "e1w1": c("L1_ffn_w1"), "e1b1": c("L1_ffn_b1").reshape(1, X * D),
        "e1w2": c("L1_ffn_w2"), "e1b2": c("L1_ffn_b2").reshape(1, X * D),
    }
    nc = bacc.Bacc("TRN2", target_bir_lowering=False, num_devices=1)
    aps = {n: nc.dram_tensor("in_" + n, v.shape, mybir.dt.from_np(v.dtype), kind="ExternalInput").ap()
           for n, v in arrays.items()}
    out = nc.dram_tensor("out", (N, D), F32, kind="ExternalOutput").ap()
    program(nc, aps, out)
    r = run(nc, [{"in_" + n: v for n, v in arrays.items()}], core_ids=[0])
    return r.results[0]["out"]
```

```python
from contextlib import ExitStack

import concourse.bass as bass
from concourse import mybir

F32 = mybir.dt.float32
F16 = mybir.dt.float16
I32 = mybir.dt.int32
ALU = mybir.AluOpType
ACT = mybir.ActivationFunctionType
AX_X = mybir.AxisListType.X

P = 128
N, D = 3125, 256
T = -(-N // P)
NP = T * P
E = 50000
C = 392
NREL, NBASES = 8, 4
KS = 416
X, TOPK = 8, 2
H0 = 682
HH = H0 // 2
HC = 114
NHC = -(-H0 // HC)
CM = TOPK * T
KM = 56
EPS = 1e-5
SKIP = 1.0e6
SKIP_SLOT = 1024.0
HG = 10
PACK = 32768
SB = 14
C_SCAT = (224, C)
PB = 4
HALF_BITS = 11
COUNT_1, COUNT_2 = 1, 9
PERM_FROM = 15
GB = 8
BPW = 4
ST = 11
TG = 5
XB = 4
SCAT_EARLY = 3
ROOT_TILES, ROOT_ROUNDS = 9, 9
PARTS, ROUNDS = -(-T // ROOT_TILES), KS // (2 * GB)
assert C * P >= E and all(c % (2 * SB) == 0 and (C - c) % (2 * PB) == 0 for c in C_SCAT) and KS % (2 * GB) == 0 and GB % BPW == 0
assert KS >= (E + T * (P - 1)) // P and KM >= (N * TOPK + X * (P - 1)) // P and T % 2 and KM % 2 == 0
assert C_SCAT[1] == SCAT_EARLY * 2 * SB + ST * KM // 2 and SB >= ST and PARTS * ROOT_ROUNDS >= ROUNDS and T % TG == 0
assert T ** BPW < 1 << 24 and P * PACK + N * NREL < 1 << 24 and NP * NREL <= PACK


def program(nc, a, out):
    rel_table = nc.dram_tensor("rel_table", [NP * NREL, D], F32)
    hn_tables = [nc.dram_tensor(f"hn_table{i}", [NP, D], F32) for i in range(3)]
    h_table = nc.dram_tensor("h_table", [NP, D], F32)
    sorted_edges = [nc.dram_tensor(f"sorted_edges{l}", [P * KS, 1], I32) for l in range(2)]
    results = nc.dram_tensor("results", [CM * P, D], F32)

    with ExitStack() as ctx:
        def sb(name, shape, dt=F32):
            return ctx.enter_context(nc.sbuf_tensor(name, shape, dt))

        def sem(name):
            return ctx.enter_context(nc.semaphore(name))

        x = sb("x", [P, T, D])
        hn = sb("hn", [P, T, D])
        consts = sb("consts", [P, 3 * P])
        ident, below, lane = (consts[:, i * P:(i + 1) * P] for i in range(3))
        ones = sb("ones", [P, P])
        small = sb("small", [P, 2 * X + T])
        choice_h = sb("choice_h", [P, P + KM + 2 * CM], F16)
        rows_h, slots_h = choice_h[:, 0:P], choice_h[:, P:P + KM]
        choice_ids = choice_h[:, P + KM:].rearrange("p (i c) -> p i c", i=2)
        iota_x, iota_x8 = small[:, 0:X], small[:, X:2 * X]
        beyond = small[:, 2 * X:2 * X + T]
        starts = sb("starts", [P, KM + BPW])
        tok_starts, word_starts = starts[0:1, 0:KM], starts[:, KM:KM + BPW]
        slot_word = sb("slot_word", [P, 2, BPW])
        slot_word_i = sb("slot_word_i", [P, 2], I32)
        bias0 = sb("bias0", [P, D])
        rw = sb("rw", [P, 2, 2, X])
        wc = sb("wc", [P, NBASES])
        gidx = sb("gidx", [P, KS], I32)
        lists = sb("lists", [P, 2 * KS], I32)
        packed, gloc_i = lists[:, 0:KS], lists[:, KS:2 * KS]
        lg = lists[:, 0:4 * T * X].bitcast(F32).rearrange("p (i t e) -> p i t e", i=4, t=T)
        gloc = sb("gloc", [P, KS])
        sort_work = sb("sort_work", [P, 2 * X * CM])
        bucket = sort_work[:, 0:2 * C].rearrange("p (l c) -> p l c", l=2)
        msort = sort_work[:, :].rearrange("p (i e c) -> p i e c", i=2, e=X)
        place = sb("place", [P, 2, C], I32)
        load = sb("load", [P, 2, C], I32)
        block_of = sb("block_of", [1, 2, KS // BPW], I32)
        expert_words = sb("expert_words", [1, KM // XB], I32)
        slot_expert = sb("slot_expert", [1, KM + 2])
        stg_place = sb("stg_place", [P, 2, SB], I32)
        stg_load = sb("stg_load", [P, 2, SB], I32)
        stg_g = sb("stg_g", [P, 2, GB], I32)
        stats = sb("stats", [P, T, 6])
        mean = sb("mean", [P, T])
        rstd = sb("rstd", [P, T])
        upto = sb("upto", [P, T + 1])
        cnt = sb("cnt", [P, 4, T])
        cnt_i = sb("cnt_i", [P, T], I32)
        hT = sb("hT", [P, 2, 2, P])
        gates = sb("gates", [P, TOPK, T])
        tops = sb("tops", [P, 2, T])
        choice = sb("choice", [P, TOPK, T])
        rank = sb("rank", [P, CM])
        place_i = sb("place_i", [P, 2, CM], I32)
        place_h = sb("place_h", [P, 2, CM], F16)
        tok_rows = sb("tok_rows", [P, KM + XB + 2, 2], I32)
        stg_tok = sb("stg_tok", [P, XB, 2], I32)
        slot_tok = sb("slot_tok", [P, 3, KM])
        deg = sb("deg", [P, 2, T])

        ARENA = 4 * X * H0 + (NHC - 1) * X * D
        arena = sb("arena", [P, ARENA])

        def at(off, *shape, dt=F32, parts=P):
            n = 1
            for d in shape:
                n *= d
            n = n // 2 if dt == F16 else n
            assert off + n <= ARENA
            v = arena[0:parts, off:off + n]
            if dt != F32:
                v = v.bitcast(dt)
            names = "abc"[:len(shape)]
            if len(shape) > 1:
                v = v.rearrange(f"p ({' '.join(names)}) -> p {' '.join(names)}", **dict(zip(names[:-1], shape)))
            return v

        hot_sort, scan_sort = at(0, T, C, dt=F16), at(T * C, T, C)
        hot_flat, scan_flat = at(0, T * C, dt=F16), at(T * C, T * C)
        basis_sb = [at(k * T * C, NREL, NBASES, D) for k in range(2)]
        w_rel = at(2 * T * C, 2, NREL, D)
        o = 2 * T * C + 2 * NREL * D
        rel_out = at(o, 2, NREL * D)
        raw = at(o, 3, C, dt=I32)
        work_i = at(o + 3 * C, 3, C, dt=I32)
        work_f = at(o + 6 * C, 2, C)
        o += 2 * NREL * D
        perm_row = at(o, 2 * PB, 2, P, dt=F16)
        perm_col = at(o + 2 * PB * P, 2 * PB, KS, dt=F16)
        o += 2 * PB * P + PB * KS
        count_h = at(o, KS + P, dt=F16)
        count_cols, count_rows = count_h[:, 0:KS], count_h[:, KS:KS + P]
        o += (KS + P) // 2
        CP = C - C_SCAT[0]
        row_of, col_of, part_a, part_b = (at(o + i * CP, CP) for i in range(4))
        part_i = at(o + 4 * CP, CP, dt=I32)
        w13 = at(0, 4, X * H0)
        o = 4 * X * H0
        gath = [[at(o + b * D, D) for b in range(2 * GB)]]
        hot = [at(o + 2 * GB * D, 2 * GB, P)]
        w2a = at(o, NHC - 1, X * D)
        acc0 = hn
        hnf = hn[:, :, :].rearrange("p a b -> p (a b)")
        xs = hnf[:, 0:XB * D].rearrange("p (j d) -> p j d", j=XB)
        o = XB * D
        xsT = hnf[:, o:o + 512].rearrange("p (j k d) -> p j k d", j=2, k=2)
        ys = hnf[:, o + 512:o + 1024].rearrange("p (j d) -> p j d", j=2)
        hid = hnf[:, o + 1024:o + 1024 + H0]
        o += 1024 + H0
        hidT = hnf[:, o:o + 2 * NHC * P].rearrange("p (j k d) -> p j k d", j=2, k=NHC)
        o += 2 * NHC * P
        w2b = hnf[:, o:o + X * D]
        w2 = [w2a[:, k, :] for k in range(NHC - 1)] + [w2b]
        y_back = at(0, CM, D)
        HOTS = CM * (P + 2 * KM) // 2
        hot_rows = [at(o, CM, P, dt=F16) for o in (ARENA - HOTS, 0)]
        hot_cols = [at(o + CM * P // 2, CM, 2 * KM, dt=F16) for o in (ARENA - HOTS, 0)]
        W2_EARLY = (ARENA - HOTS - 4 * X * H0) // (X * D)
        root = at(0, T, D)
        accx = at(T * D, T, D + 1)
        o = T * (2 * D + 1)
        acch = at(o, T, 2 * D)
        o += T * 2 * D
        g1 = at(T * (2 * D + 1), 2 * GB, D + 1)
        gath.append([g1[:, b, :] for b in range(2 * GB)])
        hot.append(at(T * (2 * D + 1) + 2 * GB * (D + 1), 2 * GB, P))
        gath.append([at(o + b * 2 * D, 2 * D) for b in range(GB)] +
                    [hnf[:, b * 2 * D:(b + 1) * 2 * D] for b in range(GB)])
        hot.append(hnf[:, GB * 2 * D:GB * (2 * D + 2 * P)].rearrange("p (b n) -> p b n", n=P))
        o += 2 * GB * D
        w_root, w_neigh, bias1 = at(o, 2, D), at(o + 2 * D, 2, D), at(o + 4 * D, D, parts=1)
        e1w1, e1w2 = at(CM * D, 2, X * D), at(CM * D + 2 * X * D, 2, X * D)
        e1b = at(CM * D + 4 * X * D, 2, X * D)
        acc = [acc0[:, :, :], accx, acch]
        width = [D, D + 1, 2 * D]

        ps = ctx.enter_context(nc.psum_tensor("ps", [P, 8, 512], F32))

        edges_in, consts_in, x_in, wc_in, bias_in, rw_in = map(
            sem, "edges_in consts_in x_in wc_in bias_in rw_in".split())
        basis_in = [sem("basis_in0"), sem("basis_in1")]
        set_pool, pad_set, zero_set, lists_init = map(
            sem, "set_pool pad_set zero_set lists_init".split())
        dve_step, ranked, counted, edges_placed, tokens_placed = map(
            sem, "dve_step ranked counted edges_placed tokens_placed".split())
        staged, list_in, list_ready = map(sem, "staged list_in list_ready".split())
        word_out, words_in, perm_out, permuted = map(sem, "word_out words_in perm_out permuted".split())
        scattered = [sem("scattered0"), sem("scattered1")]
        stat_out = sem("stat_out")
        var_out, std_out, normed, turned, turned_in, routed = map(
            sem, "var_out std_out normed turned turned_in routed".split())
        w_rel_out, rel_mm, rel_copied = map(sem, "w_rel_out rel_mm rel_copied".split())
        rel_stored = [sem("rel_stored0"), sem("rel_stored1")]
        gathered = [[sem(f"gathered{l}_{b}") for b in range(2 * GB)] for l in range(3)]
        hot_out = [sem(f"hot_out{l}") for l in range(3)]
        summed = [sem(f"summed{l}") for l in range(3)]
        added = [sem(f"added{l}") for l in range(3)]
        staged_g = [sem(f"staged_g{l}") for l in range(3)]
        squared, begun, added_first = sem("squared"), sem("begun"), sem("added_first")
        w13_in, w2_in, e1_in, wl_in = map(sem, "w13_in w2_in e1_in wl_in".split())
        lgm_out, exp_out, hots_out, tok_permuted, tok_staged = map(
            sem, "lgm_out exp_out hots_out tok_permuted tok_staged".split())
        experts_known = sem("experts_known")
        hn_stored = [sem(f"hn_stored{i}") for i in range(3)]
        xs_in = [sem(f"xs_in{j}") for j in range(XB)]
        xs_turned, xsT_in, h_mm, act_out, hid_out, hid_turned, hidT_act, hidT_dve, y_mm, y_out = map(
            sem, "xs_turned xsT_in h_mm act_out hid_out hid_turned hidT_act hidT_dve y_mm y_out".split())
        ys_stored = [sem("ys_stored0"), sem("ys_stored1")]
        back = [sem(f"back{g}") for g in range(CM // TG)]
        combined, root_mm, root_out, neigh_mm, pre_out, h_out, h_stored = map(
            sem, "combined root_mm root_out neigh_mm pre_out h_out h_stored".split())
        gg_out, tanh_out, tanh_added, out_stored = map(
            sem, "gg_out tanh_out tanh_added out_stored".split())
        passed = {e: sem(f"passed_{e}") for e in ("sp", "pool", "act", "dve", "pe")}

        def hold(e, eng, semaphore, value):
            if isinstance(value, int):
                if value > 0:
                    eng.wait_ge(semaphore, value)
            else:
                eng.wait_ge(semaphore, value)
                eng.sem_inc(passed[e], 1)

        def result_order():
            return [choice * T + t for t in range(0, T, TG) for choice in range(TOPK)]

        def pairs(eng, body):
            for t in range(3):
                body(t, t % 2)
            with eng.Fori(1, T // 2) as i:
                body(i * 2 + 1, 1)
                body(i * 2 + 2, 0)

        def rounds(eng, n, body, first=0):
            if first == 0:
                body(0)
            with eng.Fori(max(first, 1), n) as i:
                body(i)

        block = ctx.enter_context(nc.Block())

        @block.sync
        def _(sp):
            full = (T - 1) * P
            for i, name in enumerate(("src", "dst", "et")):
                sp.dma_start(raw[:, i, :], a[name]).then_inc(edges_in, 16)
            sp.dma_start(consts[:, :], a["c_mats"]).then_inc(consts_in, 16)
            sp.dma_start(small[:, :], a["c_small"]).then_inc(consts_in, 16)
            sp.dma_start(starts[:, :], a["c_starts"]).then_inc(consts_in, 16)
            sp.dma_start(count_h, a["c_count"]).then_inc(consts_in, 16)
            sp.dma_start(choice_h[:, :], a["c_choices"]).then_inc(consts_in, 16)
            sp.wait_ge(zero_set, 1)
            sp.dma_start(x[:, 0:T - 1, :], a["x"][0:full, :].rearrange("(t p) d -> p t d", p=P)
                         ).then_inc(x_in, 16)
            sp.dma_start(x[0:N - full, T - 1, :], a["x"][full:N, :]).then_inc(x_in, 16)
            for r in range(NREL):
                sp.dma_start(wc[r::NREL, :], a["w_comp"][r:r + 1, :].to_broadcast([P // NREL, NBASES])
                             ).then_inc(wc_in, 16)
            sp.dma_start(bias0[:, :], a["bias0"].to_broadcast([P, D])).then_inc(bias_in, 16)
            sp.dma_start(rw[:, :, :, :], a["rw"]).then_inc(rw_in, 16)
            bases = a["basis"].rearrange("(s q b) o -> q s (b o)", q=P // 4, b=NBASES)
            for k in range(2):
                for r in range(NREL):
                    sp.dma_start(basis_sb[k][r::NREL, :, :, :].rearrange("p a b c -> p a (b c)"),
                                 bases[k * P // NREL:(k + 1) * P // NREL]).then_inc(basis_in[k], 16)
            sp.wait_ge(pad_set, 2)
            for l, pad in ((0, packed), (1, gloc_i)):
                sp.dma_start(sorted_edges[l][:, :].rearrange("(p k) o -> p (k o)", p=P), pad
                             ).then_inc(lists_init, 16)
            def store_rel(t, j):
                hold("sp", sp, rel_copied, t * 4 + 4)
                sp.dma_start(rel_table[bass.ds(t * (P * NREL), P * NREL), :].rearrange("(p r) d -> p (r d)", r=NREL),
                             rel_out[:, j, :]).then_inc(rel_stored[j], 16)
            pairs(sp, store_rel)
            for l in range(2):
                sp.wait_ge(word_out, l + 1)
                sp.dma_start(block_of[0:1, l, :], slot_word_i[0:KS // BPW, l:l + 1]).then_inc(words_in, 16)

            def load_list(l):
                for h in range(2):
                    sp.wait_ge(scattered[h], 16 * sum(C_SCAT[0:l + 1]) // 2)
                sp.dma_start(packed, sorted_edges[l][:, :].rearrange("(p k) o -> p (k o)", p=P)
                             ).then_inc(list_in, 16)
            load_list(0)
            sp.wait_ge(permuted, CP)
            sp.wait_ge(edges_placed, 2)
            sp.wait_ge(rel_mm, 4 * T)
            for e in range(X):
                sp.wait_ge(added[0], (e + 1) * (KS // 2 // X))
                for i, name in enumerate(("w1", "w1", "w3", "w3")):
                    sp.dma_start(w13[:, i, e * H0:(e + 1) * H0], a[name][e, (i % 2) * P:(i % 2 + 1) * P, :]
                                 ).then_inc(w13_in, 16)


            def store_table(table, rows, ready, past, stored):
                for t in range(0, T, TG):
                    sp.wait_ge(ready, past + t + TG)
                    sp.dma_start(table[t * P:(t + TG) * P, :].rearrange("(t p) d -> p t d", p=P),
                                 rows[:, t:t + TG, :]).then_inc(stored, 16)

            def load_results(l):
                for j in range(2):
                    sp.wait_ge(ys_stored[j], 16 * (KM // 2) * (l + 1))
                for c in result_order():
                    whole = TG - 1 if (c + TG) % T == 0 else TG
                    sp.dma_start(y_back[:, c:c + whole, :], results[c * P:(c + whole) * P, :].rearrange("(t p) d -> p t d", p=P)
                                 ).then_inc(back[c // TG], 16)
                    if whole < TG:
                        at_ = (c + whole) * P
                        sp.dma_start(y_back[0:N - full, c + whole, :], results[at_:at_ + N - full, :]
                                     ).then_inc(back[c // TG], 16)

            store_table(hn_tables[0], hn, normed, T, hn_stored[0])
            for k in range(NHC):
                n = min(HC, H0 - k * HC)
                if k == W2_EARLY:
                    sp.wait_ge(tok_permuted, 1)
                if k == NHC - 1:
                    sp.wait_ge(tokens_placed, 1)
                    sp.wait_ge(hn_stored[0], 16 * T // TG)
                sp.dma_start(w2[k][0:n, :].rearrange("p (e d) -> p e d", e=X),
                             a["w2"][:, k * HC:k * HC + n, :].rearrange("e h d -> h e d")).then_inc(w2_in, 16)
            load_list(1)
            load_results(0)
            sp.wait_ge(combined, CM)
            for name, w in (("W_root", w_root), ("W_neigh", w_neigh)):
                sp.dma_start(w, a[name].rearrange("(k p) d -> p k d", p=P)).then_inc(wl_in, 16)
            sp.dma_start(bias1, a["bias1"]).then_inc(wl_in, 16)
            store_table(hn_tables[1], hn, normed, 2 * T, hn_stored[1])
            store_table(h_table, root, h_out, 0, h_stored)
            sp.wait_ge(tanh_added, T // TG)
            for k in range(2):
                for name, w in (("e1w1", e1w1), ("e1w2", e1w2)):
                    sp.dma_start(w[:, k, :].rearrange("p (e h) -> p e h", e=X),
                                 a[name][:, k * P:(k + 1) * P, :].rearrange("e c h -> c e h")).then_inc(e1_in, 16)
                sp.dma_start(e1b[:, k, :], a[f"e1b{k + 1}"].to_broadcast([P, X * D])).then_inc(e1_in, 16)
            store_table(hn_tables[2], hn, normed, 3 * T, hn_stored[2])
            load_results(1)
            for t in range(0, T, TG):
                sp.wait_ge(combined, CM + (t + TG) * TOPK)
                end = min(t + TG, T - 1)
                sp.dma_start(out[t * P:end * P, :].rearrange("(t p) d -> p t d", p=P), x[:, t:end, :]
                             ).then_inc(out_stored, 16)
            sp.dma_start(out[full:N, :], x[0:N - full, T - 1, :]).then_inc(out_stored, 16)
            sp.wait_ge(out_stored, 16 * (T // TG + 1))

        @block.gpsimd
        def _(pool):
            pool.memset(x[:, T - 1, :], 0.0).then_inc(zero_set, 1)
            pool.memset(ones[:, :], 1.0).then_inc(set_pool, 1)
            pool.memset(packed, 0).then_inc(pad_set, 1)
            pool.memset(gloc_i, P * PACK + N).then_inc(pad_set, 1)
            BEFORE = (0, C_SCAT[0] // SB // 2)

            def scatter_half(l, i, h, size=SB, rounds_before=None, first=0):
                before = BEFORE[l] if rounds_before is None else rounds_before
                hold("pool", pool, scattered[h], (i * size + before * SB) * 16)
                at_ = bass.ds((i * 2 + h) * size + first, size)
                pool.tensor_copy(stg_place[:, h, 0:size], place[:, l, at_]).then_inc(staged, 1)
                pool.tensor_copy(stg_load[:, h, 0:size], load[:, l, at_]).then_inc(staged, 1)
                hold("pool", pool, staged, ((i + before) * 2 + h + 1) * 2)

                def scatter(b):
                    pool.indirect_dma_start(
                        sorted_edges[l][:, :], bass.IndirectOffsetOnAxis(ap=stg_place[:, h, b:b + 1], axis=0),
                        stg_load[:, h, b:b + 1], None, bounds_check=P * KS - 1, oob_is_err=False,
                    ).then_inc(scattered[h], 16)
                return scatter

            def scatter_edges(l, n):
                pool.wait_ge(edges_placed, l + 1)

                def body(i):
                    for h in range(2):
                        scatter = scatter_half(l, i, h)
                        for b in range(SB):
                            scatter(b)
                rounds(pool, n, body)

            def gather(l, table):

                def body(i):
                    for h in range(2):
                        hold("pool", pool, staged_g[l], i * 2 + (h + 1))
                        for b in range(GB):
                            pool.indirect_dma_start(
                                gath[l][h * GB + b][:, 0:D], None, table[:, :],
                                bass.IndirectOffsetOnAxis(ap=stg_g[:, h, b:b + 1], axis=0),
                            ).then_inc(gathered[l][h * GB + b], 16)
                rounds(pool, KS // GB // 2, body)

            def slots(l):
                g = l * KM
                pool.wait_ge(tokens_placed, l + 1)
                pool.wait_ge(hn_stored[2 * l], 16 * T // TG)

                def tokens_in(index, j):
                    pool.indirect_dma_start(xs[:, j, :], None, hn_tables[2 * l][:, :],
                                            bass.IndirectOffsetOnAxis(ap=index, axis=0)).then_inc(xs_in[j], 16)

                def results_out(k, j):
                    hold("pool", pool, y_out, k + (g + 1))
                    pool.indirect_dma_start(
                        results[:, :], bass.IndirectOffsetOnAxis(ap=stg_tok[:, (j + 2) % XB, 1:2], axis=0),
                        ys[:, j % 2, :], None, bounds_check=CM * P - 1, oob_is_err=False
                    ).then_inc(ys_stored[j % 2], 16)

                def stage(k, j):
                    pool.tensor_copy(stg_tok[:, j:j + 1, :], tok_rows[:, bass.ds(k + XB, 1), :]).then_inc(tok_staged, 1)
                    hold("pool", pool, tok_staged, k + (g + 1) + 2 * l)

                def body(i, last=False):
                    for j in range(XB):
                        k = i * XB + j
                        hold("pool", pool, xs_turned, k + (g + 1))
                        hold("pool", pool, ys_stored[j % 2], (i * 2 + (j // 2 - 1 + g // 2)) * 16)
                        stage(k, j)
                        if not last:
                            tokens_in(stg_tok[:, j, 0:1], j)
                        if l == 0:
                            if j % 2 == 0:
                                scatter = scatter_half(1, i, j // 2, ST, BEFORE[1] + SCAT_EARLY, SCAT_EARLY * 2 * SB)
                            for b in (range(ST // 2), range(ST // 2, ST))[j % 2]:
                                scatter(b)
                        if not isinstance(k, int) or k >= 2:
                            results_out(k - 2, j - 2)

                for k in range(XB):
                    tokens_in(tok_rows[:, k, 0:1], k)
                n = KM // XB
                rounds(pool, n - 1, body)
                body(n - 1, last=True)
                for j in range(2):
                    pool.wait_ge(ys_stored[j], (KM // 2 - 1 + g // 2) * 16)
                    stage(KM + j, j)
                    results_out(KM - 2 + j, XB - 2 + j)

            pool.wait_ge(lists_init, 32)
            scatter_edges(0, C_SCAT[0] // SB // 2)
            pool.wait_ge(list_ready, 1)
            pool.wait_ge(rel_stored[0], 16 * (T // 2 + 1))
            pool.wait_ge(rel_stored[1], 16 * (T // 2))
            gather(0, rel_table)
            scatter_edges(1, SCAT_EARLY)
            slots(0)
            pool.wait_ge(list_ready, 2)
            pool.wait_ge(hn_stored[1], 16 * T // TG)
            gather(1, hn_tables[1])
            pool.wait_ge(h_stored, 16 * T // TG)
            gather(2, h_table)
            for t in range(0, T, TG):
                pool.wait_ge(tanh_out, t + TG)
                pool.tensor_tensor(x[:, t:t + TG, :], x[:, t:t + TG, :], accx[:, t:t + TG, 0:D], ALU.add
                                   ).then_inc(tanh_added, 1)
            slots(1)

        @block.scalar
        def _(act):
            def std(n):
                act.wait_ge(var_out, n)
                act.activation(rstd[:, :], rstd[:, :], ACT.Sqrt).then_inc(std_out, 1)

            def turn(n, used, per=1, base=0):
                def body(t, j):
                    hold("act", act, turned, t + (n * T + 1))
                    if not isinstance(t, int) or t >= 2:
                        hold("act", act, used, (t - 1) * per + base)
                    act.copy(hT[:, j, :, :].rearrange("p k d -> p (k d)"), ps[:, 6 + j, 0:D]).then_inc(turned_in, 1)
                return body

            def rel_part(t, j):
                turn(0, rel_mm, 4)(t, j)
                hold("act", act, rel_stored[j], (t - j) * 8)
                for g in range(4):
                    hold("act", act, rel_mm, t * 4 + g + 1)
                    act.copy(rel_out[:, j, g * 512:(g + 1) * 512], ps[:, g, :]).then_inc(rel_copied, 1)

            def softmax_exp(n):
                act.wait_ge(lgm_out, n)
                act.activation(lg[:, 1, :, :], lg[:, 1, :, :], ACT.Exp).then_inc(exp_out, 1)

            def experts(l):
                g = l * KM

                def xsT_copy(k, j):
                    hold("act", act, xs_turned, k + (g + 1))
                    hold("act", act, h_mm, k + (g - 1))
                    act.copy(xsT[:, j, :, :].rearrange("p k d -> p (k d)"), ps[:, 5, 0:D]).then_inc(xsT_in, 1)

                def slot(k, j, last=False):
                    hold("act", act, h_mm, k + (g + 1))
                    if l == 0:
                        hold("act", act, hid_turned, k)
                        act.activation(hid.rearrange("p (b h) -> p b h", b=2), ps[:, 0:2, 0:HH], ACT.Silu
                                       ).then_inc(act_out, 1)
                    else:
                        hold("act", act, hid_turned, k + (g - 1))
                        act.activation(hid[:, j * D:(j + 1) * D], ps[:, j, 0:D], ACT.Gelu).then_inc(hid_out, 1)
                    if not last:
                        xsT_copy(k + 1, 1 - j)
                    if l == 0:
                        hidT_copy(k, j)
                    elif not isinstance(k, int) or k:
                        hidT_copy(k - 1, 1 - j)

                def hidT_copy(k, j):
                    hold("act", act, hid_turned, k + (g + 1))
                    hold("act", act, y_mm, k + (g - 1))
                    if l == 0:
                        act.copy(hidT[0:HC, j, 0:4, :], ps[0:HC, 6, :].rearrange("p (k d) -> p k d", k=4)
                                 ).then_inc(hidT_act, 1)
                    else:
                        act.copy(hidT[:, j, 0:2, :], ps[:, 6 + j, 0:D].rearrange("p (k d) -> p k d", k=2)
                                 ).then_inc(hidT_act, 1)

                xsT_copy(0, 0)
                slot(0, 0)
                slot(1, 1)
                with act.Fori(1, KM // 2 - 1) as i:
                    slot(i * 2, 0)
                    slot(i * 2 + 1, 1)
                slot(KM - 2, 0)
                slot(KM - 1, 1, last=True)
                if l == 1:
                    hidT_copy(KM - 1, 1)

            def root_part(tiles):
                for t in tiles:
                    turn(2, root_mm)(t, t % 2)
                    if t > tiles[0]:
                        root_copy(t - 1)
                root_copy(tiles[-1])

            def root_copy(t):
                act.wait_ge(root_mm, t + 1)
                act.copy(root[:, t, :], ps[:, t % 2, 0:D]).then_inc(root_out, 1)

            def neigh_part(t, j):
                turn(3, neigh_mm)(t, j)
                if not isinstance(t, int) or t:
                    relu(t - 1)

            def relu(t):
                hold("act", act, pre_out, t + 1)
                act.activation(root[:, bass.ds(t, 1), :], root[:, bass.ds(t, 1), :], ACT.Relu).then_inc(h_out, 1)

            def stage(l, first=0, end=KS // GB // 2):

                def squares(i, h):
                    for b in range(h * GB, (h + 1) * GB):
                        hold("act", act, gathered[l][b], (i + 1) * 16)
                        act.activation(gath[l][b][:, D:2 * D], gath[l][b][:, 0:D], ACT.Square).then_inc(squared, 1)

                def body(i):
                    for h in range(2):
                        if not isinstance(i, int) or i:
                            hold("act", act, summed[l], i * (2 * GB) + (h - 1) * GB)
                        act.copy(stg_g[:, h, 0:GB], gidx[:, bass.ds((i * 2 + h) * GB, GB)]).then_inc(staged_g[l], 1)
                        if l == 2 and h == 1:
                            squares(i, 0)
                        elif l == 2 and (not isinstance(i, int) or i):
                            squares(i - 1, 1)
                if first == 0:
                    act.wait_ge(list_ready, 1 if l == 0 else 2)
                if end == 1:
                    body(0)
                else:
                    rounds(act, end, body, first)
                if l == 2:
                    squares(end - 1, 1)

            std(1)
            pairs(act, rel_part)
            stage(0)
            std(2)
            pairs(act, turn(1, routed))
            softmax_exp(1)
            experts(0)
            std(3)
            stage(1, end=1)
            for part in range(PARTS):
                root_part(range(part * ROOT_TILES, min((part + 1) * ROOT_TILES, T)))
                stage(1, part * ROOT_ROUNDS + 1, min((part + 1) * ROOT_ROUNDS + 1, ROUNDS))
            pairs(act, neigh_part)
            relu(T - 1)
            stage(2)
            for t in range(T):
                act.wait_ge(gg_out, t // TG + 1)
                act.activation(accx[:, t, 0:D], accx[:, t, 0:D], ACT.Tanh, scale=deg[:, 1, t:t + 1]).then_inc(tanh_out, 1)
            std(4)
            pairs(act, turn(4, routed, base=T))
            softmax_exp(2)
            experts(1)

        @block.tensor
        def _(pe):
            pe.wait_ge(consts_in, 80)
            pe.wait_ge(set_pool, 1)

            def count(n, buckets):
                pe.wait_ge(ranked, n)
                pe.matmul(ps[:, 4, 416:416 + buckets], below, cnt[:, 0, 0:buckets], start=True, stop=True)
                pe.matmul(ps[:, 4, 464:464 + buckets], ones[:, :], cnt[:, 0, 0:buckets], start=True, stop=True
                          ).then_inc(counted, 1)

            def turned_tiles(n, source, use, first=0, end=T, norm=None):
                def turn(t):
                    if t >= 2:
                        pe.wait_ge(turned_in, n * T + t - 1)
                    if norm is not None:
                        pe.wait_ge(normed, norm * T + t + 1)
                    for k in range(2):
                        last = pe.transpose(ps[:, 6 + t % 2, k * P:(k + 1) * P], source(t, k), ident)
                    last.then_inc(turned, 1)
                turn(first)
                for t in range(first, end):
                    if t + 1 < end:
                        turn(t + 1)
                    pe.wait_ge(turned_in, n * T + t + 1)
                    use(t, t % 2)

            def hn_half(t, k):
                return hn[:, t, k * P:(k + 1) * P]

            def rel_tile(t, j):
                for g in range(4):
                    if t:
                        pe.wait_ge(rel_copied, 4 * (t - 1) + g + 1)
                    for k in range(2):
                        last = pe.matmul(ps[:, g, :], hT[:, j, k, :],
                                         w_rel[:, k, 2 * g:2 * g + 2, :].rearrange("p a b -> p (a b)"),
                                         start=(k == 0), stop=(k == 1))
                    last.then_inc(rel_mm, 1)
                    if t >= PERM_FROM:
                        n, groups = CP // PB // 2, (T - PERM_FROM) * 4
                        q = (t - PERM_FROM) * 4 + g
                        permute(q * n // groups, (q + 1) * n // groups)
                if t in (COUNT_1, COUNT_2):
                    count(1 if t == COUNT_1 else 2, T)

            def permute(first, end):
                n = CP // PB // 2

                def body(i):
                    for h in range(2):
                        hold("pe", pe, perm_out, i * 2 + (h + 1))
                        for b in range(h * PB, (h + 1) * PB):
                            for part in range(2):
                                last = pe.matmul(ps[:, 4 + part, 0:KS], perm_row[:, b, part, :], perm_col[:, b, :],
                                                 start=(isinstance(i, int) and i == 0 and b == 0),
                                                 stop=(isinstance(i, int) and i == n - 1 and b == 2 * PB - 1))
                            last.then_inc(permuted, 1)
                for i in range(first, end):
                    body(i)

            def router_tile(l):
                def use(t, j):
                    for k in range(2):
                        last = pe.matmul(ps[:, 4, t * X:(t + 1) * X], hT[:, j, k, :], rw[:, l, k, :],
                                         start=(k == 0), stop=(k == 1))
                    last.then_inc(routed, 1)
                return use

            def root_tile(t, j):
                if t >= 2:
                    pe.wait_ge(root_out, t - 1)
                for k in range(2):
                    pe.matmul(ps[:, j, 0:D], hT[:, j, k, :], w_root[:, k, :], start=(k == 0), stop=False)
                pe.matmul(ps[:, j, 0:D], ones[0:1, :], bias1, start=False, stop=True).then_inc(root_mm, 1)

            def neigh_tile(t, j):
                if t >= 2:
                    pe.wait_ge(pre_out, t - 1)
                for k in range(2):
                    last = pe.matmul(ps[:, 2 + j, 0:D], hT[:, j, k, :], w_neigh[:, k, :], start=(k == 0), stop=(k == 1))
                last.then_inc(neigh_mm, 1)

            def edge_sums(l, first=0, end=KS // GB // 2):
                w = width[l]

                def body(i):
                    for h in range(2):
                        hold("pe", pe, hot_out[l], i * 2 + (h + 1))
                        for b in range(h * GB, (h + 1) * GB):
                            hold("pe", pe, gathered[l][b], (i + 1) * 16)
                            if l == 2:
                                hold("pe", pe, squared, i * (2 * GB) + (b + 1))
                            k = i * (2 * GB) + b
                            if not isinstance(i, int) or k >= 8:
                                hold("pe", pe, added[l], k - 7)
                            pe.matmul(ps[:, b % 8, 0:w], hot[l][:, b, :], gath[l][b][:, 0:w],
                                      start=True, stop=True).then_inc(summed[l], 1)
                rounds(pe, end, body, first)

            def place_tokens(l):
                for c in range(CM):
                    if c % HG == 0:
                        pe.wait_ge(hots_out, (l * CM + c) // HG + 1)
                    last = pe.matmul(ps[:, 5, 0:2 * KM], hot_rows[l][:, c, :], hot_cols[l][:, c, :],
                                     start=(c == 0), stop=(c == CM - 1))
                last.then_inc(tok_permuted, 1)

            def experts(l):
                g = l * KM

                def xs_turn(k, j):
                    hold("pe", pe, xs_in[j], (k - j + XB + g) * (16 // XB))
                    hold("pe", pe, xsT_in, k + g)
                    for c in range(2):
                        last = pe.transpose(ps[:, 5, c * P:(c + 1) * P], xs[:, j, c * P:(c + 1) * P], ident)
                    last.then_inc(xs_turned, 1)

                def hidden(k, j, e):
                    hold("pe", pe, xsT_in, k + (g + 1))
                    if l == 0:
                        hold("pe", pe, hid_out, k)
                        for w in range(2):
                            for b in range(2):
                                for c in range(2):
                                    last = pe.matmul(ps[:, 2 * w + b, 0:HH], xsT[:, j, c, :],
                                                     w13[:, 2 * w + c, bass.ds(e * H0 + b * HH, HH)],
                                                     start=(c == 0), stop=(c == 1))
                    else:
                        for c in range(2):
                            pe.matmul(ps[:, j, 0:D], xsT[:, j, c, :], e1w1[:, c, bass.ds(e * D, D)],
                                      start=(c == 0), stop=False)
                        last = pe.matmul(ps[:, j, 0:D], ones[0:1, :], e1b[0:1, 0, bass.ds(e * D, D)],
                                         start=False, stop=True)
                    last.then_inc(h_mm, 1)

                def results(k, j, e):
                    if l == 0 and isinstance(k, int) and k == 0:
                        pe.wait_ge(w2_in, 16 * NHC)
                    hold("pe", pe, hidT_act, k + (g + 1))
                    if l == 0:
                        hold("pe", pe, hidT_dve, k + 1)
                    hold("pe", pe, y_out, k + g)
                    if l == 0:
                        for c in range(NHC):
                            n = min(HC, H0 - c * HC)
                            last = pe.matmul(ps[:, 4, 0:D], hidT[0:n, j, c, :], w2[c][0:n, bass.ds(e * D, D)],
                                             start=(c == 0), stop=(c == NHC - 1))
                    else:
                        for c in range(2):
                            last = pe.matmul(ps[:, 4, 0:D], hidT[:, j, c, :], e1w2[:, c, bass.ds(e * D, D)],
                                             start=(c == 0), stop=(c == 1))
                    last.then_inc(y_mm, 1)

                def hidden_turn(k, j):
                    hold("pe", pe, hid_out, k + (g + 1))
                    if l == 0:
                        for c in range(NHC):
                            n = min(HC, H0 - c * HC)
                            last = pe.transpose(ps[0:n, 6 + c // 4, (c % 4) * P:(c % 4 + 1) * P],
                                                hid[:, c * HC:c * HC + n], ident)
                    else:
                        for c in range(2):
                            last = pe.transpose(ps[:, 6 + j, c * P:(c + 1) * P],
                                                hid[:, j * D + c * P:j * D + (c + 1) * P], ident)
                    last.then_inc(hid_turned, 1)

                def slots(k0, group=None, last=False):
                    word = pe.value_load(expert_words[0:1, bass.ds(k0 // XB if isinstance(k0, int) else group, 1)],
                                         min_val=0, max_val=X ** (XB + 2) - 1)

                    def expert(j):
                        return (word >> (3 * (j + 2))) & (X - 1)

                    for j in range(XB):
                        k = k0 + j
                        more = j < XB - 1 or not last
                        hidden(k, j % 2, expert(j))
                        if l == 0:
                            if not isinstance(k, int) or k:
                                results(k - 1, (j + 1) % 2, expert(j - 1))
                            if more:
                                xs_turn(k + 1, (j + 1) % XB)
                            hidden_turn(k, j % 2)
                        else:
                            if more:
                                xs_turn(k + 1, (j + 1) % XB)
                            if not isinstance(k, int) or k:
                                hidden_turn(k - 1, (j + 1) % 2)
                            if not isinstance(k, int) or k > 1:
                                results(k - 2, j % 2, expert(j - 2))
                    if last:
                        if l == 1:
                            hidden_turn(k, 1)
                            results(k - 1, 0, expert(XB - 2))
                        results(k, 1, expert(XB - 1))

                pe.wait_ge(experts_known, l + 1)
                if l == 0:
                    pe.wait_ge(w13_in, 64 * X)
                else:
                    pe.wait_ge(e1_in, 96)
                xs_turn(0, 0)
                slots(0)
                with pe.Fori(1, KM // XB - 1) as i:
                    slots(i * XB, i)
                slots(KM - XB, last=True)

            pe.wait_ge(w_rel_out, 1)
            turned_tiles(0, hn_half, rel_tile, norm=0)
            pe.wait_ge(list_ready, 1)
            edge_sums(0)
            pe.wait_ge(rw_in, 16)
            turned_tiles(1, hn_half, router_tile(0), norm=1)
            count(3, X)
            place_tokens(0)
            experts(0)
            pe.wait_ge(wl_in, 48)
            for part in range(PARTS):
                if part:
                    pe.wait_ge(added[1], part * ROOT_ROUNDS * 2 * GB)
                end = min((part + 1) * ROOT_TILES, T)
                turned_tiles(2, hn_half, root_tile, part * ROOT_TILES, end, norm=2)
                pe.wait_ge(root_out, end)
                edge_sums(1, part * ROOT_ROUNDS, min((part + 1) * ROOT_ROUNDS, ROUNDS))
            pe.wait_ge(added[1], KS)
            turned_tiles(3, lambda t, k: accx[:, t, k * P:(k + 1) * P], neigh_tile)
            edge_sums(2)
            turned_tiles(4, hn_half, router_tile(1), norm=3)
            count(4, X)
            place_tokens(1)
            experts(1)

        @block.vector
        def _(dve):
            steps = [0]

            def then(ins):
                steps[0] += 1
                ins.then_inc(dve_step, 1)
                dve.wait_ge(dve_step, steps[0])

            def also(ins):
                steps[0] += 1
                ins.then_inc(dve_step, 1)

            def over_p(row, n):
                return row.unsqueeze(2).to_broadcast([row.shape[0], row.shape[1], n])

            def over_n(row, n):
                return row.unsqueeze(1).to_broadcast([row.shape[0], n, row.shape[1]])

            def rank_items(buckets, b, c, hots, scans, hots_flat, scans_flat, result):
                for j in range(b):
                    also(dve.tensor_scalar(hots[:, j, :], buckets, float(j), None, ALU.is_equal))
                dve.wait_ge(dve_step, steps[0])
                then(dve.tensor_tensor_scan(scans_flat, hots_flat, hots_flat, 0.0, ALU.add, ALU.max))
                then(dve.tensor_copy(upto[:, 1:b + 1], scans[:, :, c - 1]))
                dve.tensor_tensor(cnt[:, 0, 0:b], upto[:, 1:b + 1], upto[:, 0:b], ALU.subtract).then_inc(ranked, 1)
                count_no[0] += 1
                dve.wait_ge(counted, count_no[0])
                then(dve.tensor_scalar(cnt_i[:, 0:b], ps[:, 4, 464:464 + b], float(P - 1), None, ALU.add))
                then(dve.tensor_scalar(cnt_i[:, 0:b], cnt_i[:, 0:b], 65535 - (P - 1), None, ALU.bitwise_and))
                then(dve.tensor_copy(cnt[:, 1, 0:b], cnt_i[:, 0:b]))
                then(dve.tensor_tensor_scan(cnt[:, 2, 0:b], cnt[:, 1, 0:b], cnt[:, 1, 0:b], 0.0, ALU.add, ALU.max))
                then(dve.tensor_tensor(cnt[:, 3, 0:b], cnt[:, 2, 0:b], cnt[:, 1, 0:b], ALU.subtract))
                then(dve.tensor_tensor(cnt[:, 3, 0:b], cnt[:, 3, 0:b], ps[:, 4, 416:416 + b], ALU.add))
                then(dve.scalar_tensor_tensor(cnt[:, 3, 0:b], cnt[:, 3, 0:b], -1.0, upto[:, 0:b], ALU.add, ALU.subtract))
                for j in range(b):
                    also(dve.scalar_tensor_tensor(scans[:, j, :], scans[:, j, :], cnt[:, 3, j:j + 1], hots[:, j, :],
                                                  ALU.add, ALU.mult))
                dve.wait_ge(dve_step, steps[0])
                then(dve.tensor_reduce(result, scans.rearrange("p b c -> p c b"), AX_X, ALU.add))

            count_no = [0]

            def slot_experts(b, n, compare, result):
                ends = cnt[0:1, 2, 0:b]
                cmp = compare.rearrange("p (k b) -> p k b", b=b)
                then(dve.tensor_tensor(cmp, over_n(ends, n), over_p(tok_starts, b), ALU.is_le))
                then(dve.tensor_reduce(scan_row[:, 0:n], cmp, AX_X, ALU.add))
                then(dve.tensor_scalar(result, scan_row[:, 0:n], float(b - 1), None, ALU.min))

            def pack_experts():
                n = KM // XB
                word = scan_row[:, 0:n]
                of = [slot_expert[:, i:i + (n - 1) * XB + 1:XB] for i in range(XB + 2)]
                then(dve.tensor_copy(word, of[-1]))
                for i in range(XB, -1, -1):
                    then(dve.scalar_tensor_tensor(word, word, float(X), of[i], ALU.mult, ALU.add))
                dve.tensor_copy(expert_words[:, :], word).then_inc(experts_known, 1)

            scan_row = gloc[0:1, :]

            def slot_blocks(l):
                cmp = scan_sort[:, 0:BPW, 0:T]
                then(dve.tensor_tensor(cmp, over_n(cnt[:, 2, 0:T], BPW), over_p(word_starts, T), ALU.is_le))
                of = slot_word[:, l, :]
                then(dve.tensor_reduce(of, cmp, AX_X, ALU.add))
                then(dve.tensor_scalar(of, of, float(T - 1), None, ALU.min))
                for j in range(BPW - 2, -1, -1):
                    then(dve.scalar_tensor_tensor(of[:, j:j + 1], of[:, j + 1:j + 2], float(T), of[:, j:j + 1],
                                                  ALU.mult, ALU.add))
                dve.tensor_copy(slot_word_i[:, l:l + 1], of[:, 0:1]).then_inc(word_out, 1)

            def read_edges():
                dve.wait_ge(edges_in, 48)
                src, dst, et = (raw[:, i, :] for i in range(3))
                for l, to in ((0, dst), (1, src)):
                    then(dve.tensor_scalar(work_i[:, 0, :], to, 7, None, ALU.logical_shift_right))
                    dve.tensor_copy(bucket[:, l, :], work_i[:, 0, :])
                    then(dve.tensor_scalar(work_i[:, 1 + l, :], to, P - 1, None, ALU.bitwise_and))
                then(dve.scalar_tensor_tensor(work_f[:, 0, :], src, float(NREL), et, ALU.mult, ALU.add))
                then(dve.tensor_scalar(work_f[:, 0, :], work_f[:, 0, :], -1.0, float(N * NREL), ALU.mult, ALU.add))
                then(dve.tensor_scalar(work_f[:, 0, :], work_f[:, 0, :], 0.0, None, ALU.max))
                then(dve.scalar_tensor_tensor(load[:, 0, :], work_i[:, 1, :], float(PACK), work_f[:, 0, :],
                                              ALU.mult, ALU.add))
                then(dve.scalar_tensor_tensor(load[:, 1, :], work_i[:, 2, :], float(PACK), dst, ALU.mult, ALU.add))

            def sort_edges(l):
                rank_items(bucket[:, l, :], T, C, hot_sort, scan_sort, hot_flat, scan_flat, sort_f[:, 0, :])
                then(dve.tensor_copy(sort_i[:, 0, :], sort_f[:, 0, :]))
                then(dve.tensor_scalar(sort_i[:, 1, :], sort_i[:, 0, :], P - 1, None, ALU.bitwise_and))
                then(dve.tensor_scalar(sort_i[:, 0, :], sort_i[:, 0, :], 7, None, ALU.logical_shift_right))
                then(dve.tensor_scalar(sort_f[:, 1, :], bucket[:, l, :], float(T), SKIP, ALU.is_ge, ALU.mult))
                if l == 0:
                    rest = slice(C_SCAT[0], C)
                    then(dve.tensor_copy(row_of, sort_i[:, 1, rest]))
                    then(dve.tensor_tensor(col_of, sort_i[:, 0, rest], sort_f[:, 1, rest], ALU.add))
                    then(dve.tensor_scalar(part_i, load[:, 0, rest], HALF_BITS, None, ALU.logical_shift_right))
                    then(dve.tensor_copy(part_a, part_i))
                    then(dve.tensor_scalar(part_i, load[:, 0, rest], (1 << HALF_BITS) - 1, None, ALU.bitwise_and))
                    then(dve.tensor_copy(part_b, part_i))
                then(dve.scalar_tensor_tensor(sort_f[:, 0, :], sort_i[:, 1, :], float(KS), sort_i[:, 0, :],
                                              ALU.mult, ALU.add))
                then(dve.tensor_tensor(place[:, l, :], sort_f[:, 0, :], sort_f[:, 1, :], ALU.add))
                dve.sem_inc(edges_placed, 1)
                slot_blocks(l)

            def permute():
                def body(i):
                    for h in range(2):
                        if not isinstance(i, int) or i:
                            hold("dve", dve, permuted, i * (2 * PB) + (h - 1) * PB)
                        for b in range(h * PB, (h + 1) * PB):
                            c = bass.ds(i * (2 * PB) + b, 1)
                            dve.tensor_scalar(perm_col[:, b, :], count_cols, col_of[:, c], None, ALU.is_equal)
                            for part, of in enumerate((part_a, part_b)):
                                last = dve.tensor_scalar(perm_row[:, b, part, :], count_rows, row_of[:, c], of[:, c],
                                                         ALU.is_equal, ALU.mult)
                        last.then_inc(perm_out, 1)
                rounds(dve, CP // PB // 2, body)

            sort_f = at(0, 2, C)
            sort_i = at(2 * C, 2, C, dt=I32)

            def relation_weights():
                dve.wait_ge(wc_in, 16 * NREL)
                for k in range(2):
                    dve.wait_ge(basis_in[k], 16 * NREL)
                    then(dve.tensor_scalar(w_rel[:, k, :, :], basis_sb[k][:, :, 0, :], wc[:, 0:1], None, ALU.mult))
                    for b in range(1, NBASES):
                        then(dve.scalar_tensor_tensor(w_rel[:, k, :, :], basis_sb[k][:, :, b, :], wc[:, b:b + 1],
                                                      w_rel[:, k, :, :], ALU.mult, ALU.add))
                dve.sem_inc(w_rel_out, 1)

            def layer_norm(n):
                U = TG
                with dve.Fori(0, T // U) as i:
                    if n == 4:
                        hold("dve", dve, tanh_added, i + 1)
                    for u in range(U):
                        t = i * U + u
                        dve.bn_stats(stats[:, bass.ds(t, 1), :].rearrange("p a b -> p (a b)"),
                                     x[:, bass.ds(t, 1), :].rearrange("p a b -> p (a b)")).then_inc(stat_out, 1)
                dve.wait_ge(stat_out, n * T)
                then(dve.tensor_tensor(mean[:, :], stats[:, :, 1], stats[:, :, 4], ALU.add))
                then(dve.tensor_tensor(rstd[:, :], stats[:, :, 1], stats[:, :, 4], ALU.subtract))
                then(dve.tensor_tensor(rstd[:, :], rstd[:, :], rstd[:, :], ALU.mult))
                then(dve.tensor_scalar(rstd[:, :], rstd[:, :], 0.25, EPS, ALU.mult, ALU.add))
                then(dve.tensor_tensor(stats[:, :, 2], stats[:, :, 2], stats[:, :, 5], ALU.add))
                then(dve.scalar_tensor_tensor(rstd[:, :], stats[:, :, 2], 1.0 / D, rstd[:, :], ALU.mult, ALU.add))
                dve.tensor_scalar(mean[:, :], mean[:, :], 0.5, None, ALU.mult).then_inc(var_out, 1)
                dve.wait_ge(std_out, n)
                then(dve.reciprocal(rstd[:, :], rstd[:, :]))
                with dve.Fori(0, T // U) as i:
                    for u in range(U):
                        t = bass.ds(i * U + u, 1)
                        dve.tensor_scalar(hn[:, t, :], x[:, t, :], mean[:, t], rstd[:, t],
                                          ALU.subtract, ALU.mult).then_inc(normed, 1)

            def unpack(l):
                dve.wait_ge(list_in, 16 * (l + 1))
                if l == 0:
                    dve.wait_ge(permuted, CP)
                    then(dve.tensor_copy(gloc[:, :], packed))
                    then(dve.tensor_tensor(gloc[:, :], gloc[:, :], ps[:, 5, 0:KS], ALU.add))
                    then(dve.scalar_tensor_tensor(packed, ps[:, 4, 0:KS], float(1 << HALF_BITS), gloc[:, :],
                                                  ALU.mult, ALU.add))
                then(dve.tensor_scalar(gidx[:, :], packed, PACK - 1, None, ALU.bitwise_and))
                if l == 0:
                    then(dve.tensor_scalar(gidx[:, :], gidx[:, :], -1.0, float(N * NREL), ALU.mult, ALU.add))
                then(dve.tensor_scalar(gloc_i, packed, 15, None, ALU.logical_shift_right))
                then(dve.tensor_copy(gloc[:, :], gloc_i))
                dve.sem_inc(list_ready, 1)

            def edge_sums(l):
                w, lst = width[l], min(l, 1)

                def one_hot(i, h):
                    if not isinstance(i, int) or i:
                        hold("dve", dve, summed[l], i * (2 * GB) + (h - 1) * GB)
                    nodes = gloc[:, bass.ds((i * 2 + h) * GB, GB)]
                    dve.tensor_tensor(hot[l][:, h * GB:(h + 1) * GB, :], over_n(lane, GB), over_p(nodes, P),
                                      ALU.is_equal).then_inc(hot_out[l], 1)

                def add(i, h):
                    for b in range(h * GB, (h + 1) * GB):
                        k = i * (2 * GB) + b
                        if b % BPW == 0:
                            word = i * (2 * GB // BPW) + b // BPW
                            blocks = dve.value_load(block_of[0:1, lst, bass.ds(word, 1)], min_val=0, max_val=T ** BPW - 1)
                            hold("dve", dve, summed[l], k + BPW)
                        blk = (blocks // T ** (b % BPW)) % T
                        halves = ((0, D, added_first), (D, w, added[l])) if l == 2 else ((0, w, added[l]),)
                        for lo, hi, done in halves:
                            hold("dve", dve, done, k)
                            to = acc[l][:, bass.ds(blk, 1), lo:hi]
                            dve.tensor_tensor(to, to, ps[:, b % 8:b % 8 + 1, lo:hi], ALU.add).then_inc(done, 1)

                def body(i):
                    one_hot(i, 0)
                    if not isinstance(i, int) or i:
                        add(i - 1, 1)
                    one_hot(i, 1)
                    add(i, 0)
                n = KS // GB // 2
                rounds(dve, n, body)
                add(n - 1, 1)
                dve.wait_ge(added[l], KS)
                if l == 2:
                    dve.wait_ge(added_first, KS)

            def route(l):
                flat = [lg[:, i, :, :] for i in range(4)]
                dve.wait_ge(routed, (l + 1) * T)
                then(dve.tensor_copy(flat[0].rearrange("p a b -> p (a b)"), ps[:, 4, 0:T * X]))
                then(dve.tensor_reduce(tops[:, 0, :], flat[0], AX_X, ALU.max))
                dve.tensor_tensor(flat[1], flat[0], over_p(tops[:, 0, :], X), ALU.subtract).then_inc(lgm_out, 1)
                dve.wait_ge(exp_out, l + 1)
                then(dve.tensor_reduce(tops[:, 0, :], flat[1], AX_X, ALU.add))
                then(dve.reciprocal(tops[:, 0, :], tops[:, 0, :]))
                then(dve.tensor_tensor(flat[1], flat[1], over_p(tops[:, 0, :], X), ALU.mult))
                for c in range(TOPK):
                    then(dve.tensor_reduce(gates[:, c, :], flat[1], AX_X, ALU.max))
                    then(dve.tensor_tensor(flat[2], flat[1], over_p(gates[:, c, :], X), ALU.is_equal))
                    then(dve.scalar_tensor_tensor(flat[2], flat[2], -float(X), over_n(iota_x8, T), ALU.mult, ALU.add))
                    then(dve.tensor_reduce(choice[:, c, :], flat[2], AX_X, ALU.min))
                    if c + 1 < TOPK:
                        then(dve.tensor_tensor(flat[2], over_n(iota_x, T), over_p(choice[:, c, :], X), ALU.is_equal))
                        then(dve.scalar_tensor_tensor(flat[1], flat[2], -2.0, flat[1], ALU.mult, ALU.add))
                then(dve.tensor_tensor(tops[:, 1, :], gates[:, 0, :], gates[:, 1, :], ALU.add))
                if l == 0:
                    then(dve.tensor_scalar(tops[:, 1, :], tops[:, 1, :], 1e-9, None, ALU.add))
                else:
                    then(dve.tensor_scalar(tops[:, 1, :], tops[:, 1, :], 1e-12, None, ALU.max))
                then(dve.reciprocal(tops[:, 1, :], tops[:, 1, :]))
                then(dve.tensor_tensor(gates[:, :, :], gates[:, :, :], over_n(tops[:, 1, :], TOPK), ALU.mult))
                then(dve.tensor_tensor(choice[:, :, :], choice[:, :, :], over_n(beyond, TOPK), ALU.add))
                ch = choice[:, :, :].rearrange("p a b -> p (a b)")
                m0, m1 = (msort[:, i, :, :] for i in range(2))
                rank_items(ch, X, CM, m0, m1, m0.rearrange("p a b -> p (a b)"), m1.rearrange("p a b -> p (a b)"),
                           rank[:, :])
                then(dve.tensor_scalar(ch, ch, float(X), SKIP_SLOT, ALU.is_ge, ALU.mult))
                then(dve.tensor_copy(place_i[:, 0, :], rank[:, :]))
                then(dve.tensor_scalar(place_i[:, 1, :], place_i[:, 0, :], 7, None, ALU.logical_shift_right))
                then(dve.tensor_scalar(place_i[:, 0, :], place_i[:, 0, :], P - 1, None, ALU.bitwise_and))
                then(dve.tensor_copy(place_h[:, 0, :], place_i[:, 0, :]))
                then(dve.tensor_tensor(place_h[:, 1, :], place_i[:, 1, :], ch, ALU.add))
                for c in range(0, CM, HG):
                    cs = slice(c, c + HG)
                    cols = hot_cols[l][:, cs, :].rearrange("p c (i k) -> p i c k", i=2)
                    also(dve.tensor_tensor(hot_rows[l][:, cs, :], over_n(rows_h, HG), over_p(place_h[:, 0, cs], P),
                                           ALU.is_equal))
                    then(dve.tensor_tensor(cols[:, 0], over_n(slots_h, HG), over_p(place_h[:, 1, cs], KM), ALU.is_equal))
                    also(dve.tensor_tensor(cols[:, 1], cols[:, 0], over_p(choice_ids[:, 1, cs], KM), ALU.mult))
                    dve.wait_ge(dve_step, steps[0])
                    dve.tensor_tensor(cols[:, 0], cols[:, 0], over_p(choice_ids[:, 0, cs], KM), ALU.mult
                                      ).then_inc(hots_out, 1)
                if l == 1:
                    dve.wait_ge(normed, 4 * T)
                    then(dve.tensor_tensor(x[:, :, :], x[:, :, :], hn[:, :, :], ALU.add))
                cm2 = msort[0:1, :, :, :].rearrange("p j a b -> p (j a b)")[:, 0:KM * X]
                slot_experts(X, KM, cm2, slot_expert[:, 2:])
                dve.wait_ge(tok_permuted, l + 1)
                ids, empty, back_to = (slot_tok[:, i, :] for i in range(3))
                then(dve.tensor_scalar(empty, ps[:, 5, KM:2 * KM], 0.0, SKIP, ALU.is_equal, ALU.mult))
                then(dve.tensor_copy(ids, ps[:, 5, KM:2 * KM]))
                then(dve.scalar_tensor_tensor(ids, ps[:, 5, 0:KM], float(P), ids, ALU.mult, ALU.add))
                also(dve.scalar_tensor_tensor(tok_rows[:, XB + 2:, 1], ids, -1.0, empty, ALU.add, ALU.add))
                then(dve.tensor_scalar(back_to, ids, NP + 1.0, float(NP), ALU.is_ge, ALU.mult))
                then(dve.scalar_tensor_tensor(back_to, ids, -1.0, back_to, ALU.add, ALU.subtract))
                then(dve.tensor_scalar(tok_rows[:, 0:KM, 0], back_to, 0.0, None, ALU.max))
                dve.sem_inc(tokens_placed, 1)
                pack_experts()

            def biased_results():
                dve.wait_ge(e1_in, 96)
                dve.wait_ge(experts_known, 2)

                def group(k0, number):
                    word = dve.value_load(expert_words[0:1, bass.ds(number, 1)], min_val=0, max_val=X ** (XB + 2) - 1)
                    for j in range(XB):
                        e = (word >> (3 * (j + 2))) & (X - 1)
                        k = k0 + j
                        hold("dve", dve, y_mm, k + (KM + 1))
                        hold("dve", dve, ys_stored[j % 2], (k - j % 2 + KM) * 8)
                        dve.tensor_tensor(ys[:, j % 2, :], ps[:, 4, 0:D], e1b[:, 1, bass.ds(e * D, D)], ALU.add
                                          ).then_inc(y_out, 1)
                with dve.Fori(0, KM // XB) as i:
                    group(i * XB, i)

            def gated_hidden():
                def slot(k, j, first=False):
                    hold("dve", dve, act_out, k + 1)
                    dve.tensor_tensor(hid.rearrange("p (b h) -> p b h", b=2), hid.rearrange("p (b h) -> p b h", b=2),
                                      ps[:, 2:4, 0:HH], ALU.mult).then_inc(hid_out, 1)
                    if not first:
                        result(k - 1, 1 - j)
                    hold("dve", dve, hid_turned, k + 1)
                    hold("dve", dve, y_mm, k - 1)
                    dve.tensor_copy(hidT[0:HC, j, 4:NHC, :],
                                    ps[0:HC, 7, 0:(NHC - 4) * P].rearrange("p (k d) -> p k d", k=NHC - 4)
                                    ).then_inc(hidT_dve, 1)

                def result(k, j):
                    hold("dve", dve, y_mm, k + 1)
                    hold("dve", dve, ys_stored[j], (k - j) * 8)
                    dve.tensor_copy(ys[:, j, :], ps[:, 4, 0:D]).then_inc(y_out, 1)
                slot(0, 0, first=True)
                slot(1, 1)
                with dve.Fori(1, KM // 2) as i:
                    slot(i * 2, 0)
                    slot(i * 2 + 1, 1)
                result(KM - 1, 1)

            def combine(l):
                done = l * CM
                for c0 in result_order():
                    parts = 2 if (c0 + TG) % T == 0 else 1
                    dve.wait_ge(back[c0 // TG], 16 * parts * (l + 1))
                    if c0 >= T:
                        dve.wait_ge(combined, done)
                    for c in range(c0, c0 + TG):
                        t, n = c % T, P if (c + 1) % T else N - (T - 1) * P
                        dve.scalar_tensor_tensor(x[0:n, t, :], y_back[0:n, c, :], gates[0:n, c // T, t:t + 1],
                                                 x[0:n, t, :], ALU.mult, ALU.add).then_inc(combined, 1)
                        done += 1
                dve.wait_ge(combined, (l + 1) * CM)

            dve.wait_ge(consts_in, 80)
            then(dve.memset(upto[:, :], 0.0))
            then(dve.memset(slot_expert[:, :], 0.0))
            then(dve.memset(tok_rows[:, :, :], 0))
            read_edges()
            dve.wait_ge(x_in, 32)
            layer_norm(1)
            relation_weights()
            sort_edges(0)
            sort_edges(1)
            permute()
            dve.wait_ge(words_in, 32)
            dve.wait_ge(turned_in, T)
            dve.wait_ge(bias_in, 16)
            then(dve.tensor_copy(acc0[:, :, :], over_n(bias0[:, :], T)))
            unpack(0)
            edge_sums(0)
            then(dve.scalar_tensor_tensor(x[:, :, :], acc0[:, :, :], 0.0, x[:, :, :], ALU.max, ALU.add))
            layer_norm(2)
            route(0)
            gated_hidden()
            combine(0)
            layer_norm(3)
            then(dve.memset(accx, 0.0))
            then(dve.memset(g1[:, :, D:D + 1], 1.0))
            unpack(1)
            edge_sums(1)
            then(dve.tensor_copy(deg[:, 0, :], accx[:, :, D]))
            then(dve.tensor_scalar(deg[:, 1, :], deg[:, 0, :], 1.0, None, ALU.max))
            then(dve.reciprocal(deg[:, 1, :], deg[:, 1, :]))
            dve.wait_ge(root_out, T)

            def begin_sums(t):
                dve.wait_ge(h_out, t + 1)
                dve.scalar_tensor_tensor(acch[:, t, D:2 * D], root[:, t, :], deg[:, 0, t:t + 1], root[:, t, :],
                                         ALU.mult, ALU.mult).then_inc(begun, 1)

            dve.memset(acch[:, :, 0:D], 0.0).then_inc(begun, 1)
            for t in range(T):
                dve.wait_ge(neigh_mm, t + 1)
                dve.scalar_tensor_tensor(root[:, t, :], ps[:, 2 + t % 2, 0:D], deg[:, 1, t:t + 1], root[:, t, :],
                                         ALU.mult, ALU.add).then_inc(pre_out, 1)
                if t >= 2:
                    begin_sums(t - 2)
            begin_sums(T - 2)
            begin_sums(T - 1)
            dve.wait_ge(begun, T + 1)
            edge_sums(2)
            dve.wait_ge(h_stored, 16 * T // TG)
            for t in range(0, T, TG):
                tiles = slice(t, t + TG)
                g = accx[:, tiles, 0:D]
                then(dve.scalar_tensor_tensor(g, acch[:, tiles, 0:D], -2.0, root[:, tiles, :], ALU.mult, ALU.mult))
                dve.tensor_tensor(g, g, acch[:, tiles, D:2 * D], ALU.add).then_inc(gg_out, 1)
            layer_norm(4)
            route(1)
            biased_results()
            combine(1)


def kernel(**inputs):
    import numpy as np
    import concourse.bacc as bacc
    from concourse.bass_utils import run_bass_kernel_spmd as run

    def c(name):
        return np.ascontiguousarray(inputs[name])

    def edges(name, fill):
        v = np.full(P * C, fill, np.int32)
        v[:E] = inputs[name]
        return v.reshape(P, C)

    i = np.arange(P)
    tiles = np.arange(T)
    small = np.concatenate([
        np.broadcast_to(np.arange(X), (P, X)), np.broadcast_to(np.arange(X) + X, (P, X)),
        np.where(tiles[None, :] * P + i[:, None] >= N, 100, 0)], 1).astype(np.float32)
    of_choices = np.concatenate([np.broadcast_to(np.concatenate([i, np.arange(KM), np.arange(CM)]), (P, P + KM + CM)),
                                 np.broadcast_to(i[:, None] + 1, (P, CM))], 1).astype(np.float16)
    rw = np.stack([c("L0_ffn_router_w"), c("L1_ffn_router_w")])
    arrays = {
        "x": c("x"), "src": edges("src", NP), "dst": edges("dst", NP), "et": edges("edge_type_8", 0),
        "c_mats": np.concatenate([np.eye(P), i[:, None] < i[None, :], np.broadcast_to(i, (P, P))], 1).astype(np.float32),
        "c_small": small, "c_choices": of_choices,
        "c_starts": np.concatenate([np.broadcast_to(np.arange(KM), (P, KM)),
                                    i[:, None] * BPW + np.arange(BPW)], 1).astype(np.float32) * P,
        "c_count": np.broadcast_to(np.concatenate([np.arange(KS), i]), (P, KS + P)).astype(np.float16),
        "basis": c("L0_gnn_basis").reshape(NBASES * D, D), "w_comp": c("L0_gnn_w_comp"),
        "bias0": c("L0_gnn_bias").reshape(1, D), "bias1": c("L1_gnn_b").reshape(1, D),
        "rw": np.ascontiguousarray(rw.reshape(2, X, 2, P).transpose(3, 0, 2, 1)),
        "w1": np.ascontiguousarray(c("L0_ffn_w1").transpose(0, 2, 1)),
        "w3": np.ascontiguousarray(c("L0_ffn_w3").transpose(0, 2, 1)),
        "w2": np.ascontiguousarray(c("L0_ffn_w2").transpose(0, 2, 1)),
        "W_root": c("L1_gnn_W_root"), "W_neigh": c("L1_gnn_W_neigh"),
        "e1w1": c("L1_ffn_w1"), "e1b1": c("L1_ffn_b1").reshape(1, X * D),
        "e1w2": c("L1_ffn_w2"), "e1b2": c("L1_ffn_b2").reshape(1, X * D),
    }
    nc = bacc.Bacc("TRN2", target_bir_lowering=False, num_devices=1)
    aps = {n: nc.dram_tensor("in_" + n, v.shape, mybir.dt.from_np(v.dtype), kind="ExternalInput").ap()
           for n, v in arrays.items()}
    out = nc.dram_tensor("out", (N, D), F32, kind="ExternalOutput").ap()
    program(nc, aps, out)
    r = run(nc, [{"in_" + n: v for n, v in arrays.items()}], core_ids=[0])
    return r.results[0]["out"]
```
